# Optimizing a Trainium2 kernel written in Bass

```python
import numpy as np
import jax
import jax.numpy as jnp

def _softmax(x, axis=-1):
    return jax.nn.softmax(x, axis=axis)

def _gelu(x):
    return jax.nn.gelu(x, approximate=True)

def _silu(x):
    return jax.nn.silu(x)

def _sigmoid(x):
    return jax.nn.sigmoid(x)

def _layernorm(x, axis=-1, eps=1e-05):
    m = jnp.mean(x, axis=axis, keepdims=True)
    v = jnp.var(x, axis=axis, keepdims=True)
    return (x - m) / jnp.sqrt(v + eps)

def _scatter_add(tgt, idx, src, axis=0):
    return tgt.at[idx].add(src)

def _segment_sum(src, seg, n):
    return jax.ops.segment_sum(src, seg, n)
kernel_name = 'mk_cond_resid_d2_seqx_r8_90deb9'

def setup_inputs(seed: int=0):
    np.random.seed(seed)
    _w = jnp.asarray

    def _rec_inputs():
        import jax
        import jax.numpy as jnp
        _rk = jax.random.key(seed)
        x = 7.22e-05 + 1 * jax.random.normal(jax.random.fold_in(_rk, 1), (2, 512, 128), jnp.float32)
        _lenS = 512 - jax.random.randint(jax.random.fold_in(_rk, 7), (2,), 0, max(1, 512 // 4) + 1, jnp.int32)
        _lenS2 = 512 - jax.random.randint(jax.random.fold_in(_rk, 8), (2,), 0, max(1, 512 // 4) + 1, jnp.int32)
        cond_64 = -0.104238 + 1.01173 * jax.random.normal(jax.random.fold_in(_rk, 11), (2, 64), jnp.float32)
        fside_16xSxS_0 = -5.72187e-05 + 0.999849 * jax.random.normal(jax.random.fold_in(_rk, 12), (16, 512, 512), jnp.float32)
        _validS = jnp.arange(512)[None, :] < _lenS[:, None]
        _validS2 = jnp.arange(512)[None, :] < _lenS2[:, None]
        _causal = jnp.tril(jnp.ones((512, 512), dtype=bool))
        mask_BxS_bk0 = jnp.logical_not(jnp.broadcast_to(_validS[:, :], (2, 512)))
        return (x, cond_64, fside_16xSxS_0, mask_BxS_bk0)
    x, cond_64, fside_16xSxS_0, mask_BxS_bk0 = _rec_inputs()

    def _L0_cond_setup():
        import jax, jax.numpy as jnp
        import numpy as np
        B, S, H = (4, 256, 128)
        E = 8
        M = 64
        K = 2
        N_SHARED = 2
        SM = M * N_SHARED
        G = 64
        GE_TEMP = 1.0
        ALPHA = 0.001
        SEQ_AUX = True
        NORM_TOPK = True
        COS_TEMP = 0.78
        CONS_ALPHA = 0.01
        LEAKY_SLOPE = 0.01
        EPS_COS = 1e-08

        def _leaky(x):
            return jnp.where(x >= 0, x, LEAKY_SLOPE * x)

        def _moe_forward(hidden_states, g, wt, wg, w_gate, w_up, w_down, sw_gate, sw_up, sw_down):
            b, s, h = hidden_states.shape
            x = hidden_states.reshape(-1, h)
            T = x.shape[0]
            logits_h = x @ wt.T
            logits_g = g @ wg.T
            logits_g = jnp.repeat(logits_g, s, axis=0)
            logits = (logits_h + logits_g / GE_TEMP) / (1.0 + 1.0 / GE_TEMP)
            scores = jax.nn.softmax(logits, axis=-1)
            topk_w, topk_idx = jax.lax.top_k(scores, K)
            if K > 1 and NORM_TOPK:
                topk_w = topk_w / (topk_w.sum(-1, keepdims=True) + 1e-20)
            onehot = jax.nn.one_hot(topk_idx.reshape(b, s * K), E, dtype=jnp.float32)
            ce = onehot.sum(1) / (s * K / E)
            aux_loss = (ce * scores.reshape(b, s, E).mean(1)).sum(1).mean() * ALPHA
            gp = _leaky(jnp.einsum('th,ehm->etm', x, w_gate))
            up = jnp.einsum('th,ehm->etm', x, w_up)
            y_all = jnp.einsum('etm,emh->eth', gp * up, w_down)
            y_sel = y_all[topk_idx, jnp.arange(T)[:, None], :]
            y = (y_sel * topk_w[..., None]).sum(1).reshape(b, s, h)
            p = _leaky(hidden_states @ sw_gate) * (hidden_states @ sw_up) @ sw_down
            y = y + p
            num = jnp.sum(y * p, -1)
            den = jnp.maximum(jnp.linalg.norm(y, axis=-1), EPS_COS) * jnp.maximum(jnp.linalg.norm(p, axis=-1), EPS_COS)
            closs = CONS_ALPHA * jnp.mean(num / den / (1.0 + COS_TEMP))
            return (y, aux_loss + closs)
        key = jax.random.key(seed)
        ks = jax.random.split(key, 12)
        sh = 1.0 / np.sqrt(H)
        sm = 1.0 / np.sqrt(M)
        ssm = 1.0 / np.sqrt(SM)
        sg = 1.0 / np.sqrt(G)
        return {'hidden_states': jax.random.normal(ks[0], (B, S, H), jnp.float32), 'g': jax.random.normal(ks[1], (B, G), jnp.float32), 'wt': jax.random.uniform(ks[2], (E, H), jnp.float32, -sh, sh), 'wg': jax.random.uniform(ks[3], (E, G), jnp.float32, -sg, sg), 'w_gate': jax.random.uniform(ks[4], (E, H, M), jnp.float32, -sh, sh), 'w_up': jax.random.uniform(ks[5], (E, H, M), jnp.float32, -sh, sh), 'w_down': jax.random.uniform(ks[6], (E, M, H), jnp.float32, -sm, sm), 'sw_gate': jax.random.uniform(ks[7], (H, SM), jnp.float32, -sh, sh), 'sw_up': jax.random.uniform(ks[8], (H, SM), jnp.float32, -sh, sh), 'sw_down': jax.random.uniform(ks[9], (SM, H), jnp.float32, -ssm, ssm)}
    _L0_cond_all = _L0_cond_setup()
    _L0_cond_in = {k: v for k, v in _L0_cond_all.items() if k in ('wt', 'wg', 'w_gate', 'w_up', 'w_down', 'sw_gate', 'sw_up', 'sw_down')}
    del _L0_cond_all

    def _L1_cond_setup():
        import jax, jax.numpy as jnp
        import numpy as np
        B, N, DIM, H, DH = (2, 256, 128, 16, 64)
        INNER = H * DH
        EPS = 1e-05

        def layernorm(x, g):
            mean = jnp.mean(x, axis=-1, keepdims=True)
            var = jnp.var(x, axis=-1, keepdims=True)
            return (x - mean) * jax.lax.rsqrt(var + EPS) * g
        key = jax.random.key(seed)
        ks = jax.random.split(key, 10)
        x = jax.random.normal(ks[0], (B, N, DIM), dtype=jnp.float32)
        attn_bias = jax.random.normal(ks[1], (H, N, N), dtype=jnp.float32)
        mask = jax.random.randint(ks[2], (B, N), 0, 2).astype(bool)
        g_in = jnp.ones((DIM,), dtype=jnp.float32)
        null_attn_bias = jax.random.normal(ks[3], (H,), dtype=jnp.float32)
        null_kv = jax.random.normal(ks[4], (2, DH), dtype=jnp.float32)
        Wq = jax.random.normal(ks[5], (DIM, INNER), dtype=jnp.float32) * 0.02
        Wkv = jax.random.normal(ks[6], (DIM, 2 * DH), dtype=jnp.float32) * 0.02
        Wo = jax.random.normal(ks[7], (INNER, DIM), dtype=jnp.float32) * 0.02
        g_out = jnp.ones((DIM,), dtype=jnp.float32)
        return {'x': x, 'attn_bias': attn_bias, 'mask': mask, 'g_in': g_in, 'null_attn_bias': null_attn_bias, 'null_kv': null_kv, 'Wq': Wq, 'Wkv': Wkv, 'Wo': Wo, 'g_out': g_out}
    _L1_cond_all = _L1_cond_setup()
    _L1_cond_in = {k: v for k, v in _L1_cond_all.items() if k in ('g_in', 'null_attn_bias', 'Wq', 'Wkv', 'Wo', 'g_out')}
    del _L1_cond_all
    return {'x': x, 'cond_64': cond_64, 'fside_16xSxS_0': fside_16xSxS_0, 'mask_BxS_bk0': mask_BxS_bk0, 'L0_cond_wt': _L0_cond_in['wt'], 'L0_cond_wg': _L0_cond_in['wg'], 'L0_cond_w_gate': _L0_cond_in['w_gate'], 'L0_cond_w_up': _L0_cond_in['w_up'], 'L0_cond_w_down': _L0_cond_in['w_down'], 'L0_cond_sw_gate': _L0_cond_in['sw_gate'], 'L0_cond_sw_up': _L0_cond_in['sw_up'], 'L0_cond_sw_down': _L0_cond_in['sw_down'], 'L1_cond_g_in': _L1_cond_in['g_in'], 'L1_cond_null_attn_bias': _L1_cond_in['null_attn_bias'], 'L1_cond_Wq': _L1_cond_in['Wq'], 'L1_cond_Wkv': _L1_cond_in['Wkv'], 'L1_cond_Wo': _L1_cond_in['Wo'], 'L1_cond_g_out': _L1_cond_in['g_out']}

def reference(x, cond_64, fside_16xSxS_0, mask_BxS_bk0, L0_cond_wt, L0_cond_wg, L0_cond_w_gate, L0_cond_w_up, L0_cond_w_down, L0_cond_sw_gate, L0_cond_sw_up, L0_cond_sw_down, L1_cond_g_in, L1_cond_null_attn_bias, L1_cond_Wq, L1_cond_Wkv, L1_cond_Wo, L1_cond_g_out):
    import jax
    import jax.numpy as jnp

    def _L0_cond_ref(hidden_states, g, wt, wg, w_gate, w_up, w_down, sw_gate, sw_up, sw_down):
        import jax, jax.numpy as jnp
        import numpy as np
        B, S, H = (4, 256, 128)
        E = 8
        M = 64
        K = 2
        N_SHARED = 2
        SM = M * N_SHARED
        G = 64
        GE_TEMP = 1.0
        ALPHA = 0.001
        SEQ_AUX = True
        NORM_TOPK = True
        COS_TEMP = 0.78
        CONS_ALPHA = 0.01
        LEAKY_SLOPE = 0.01
        EPS_COS = 1e-08

        def _leaky(x):
            return jnp.where(x >= 0, x, LEAKY_SLOPE * x)

        def _moe_forward(hidden_states, g, wt, wg, w_gate, w_up, w_down, sw_gate, sw_up, sw_down):
            b, s, h = hidden_states.shape
            x = hidden_states.reshape(-1, h)
            T = x.shape[0]
            logits_h = x @ wt.T
            logits_g = g @ wg.T
            logits_g = jnp.repeat(logits_g, s, axis=0)
            logits = (logits_h + logits_g / GE_TEMP) / (1.0 + 1.0 / GE_TEMP)
            scores = jax.nn.softmax(logits, axis=-1)
            topk_w, topk_idx = jax.lax.top_k(scores, K)
            if K > 1 and NORM_TOPK:
                topk_w = topk_w / (topk_w.sum(-1, keepdims=True) + 1e-20)
            onehot = jax.nn.one_hot(topk_idx.reshape(b, s * K), E, dtype=jnp.float32)
            ce = onehot.sum(1) / (s * K / E)
            aux_loss = (ce * scores.reshape(b, s, E).mean(1)).sum(1).mean() * ALPHA
            gp = _leaky(jnp.einsum('th,ehm->etm', x, w_gate))
            up = jnp.einsum('th,ehm->etm', x, w_up)
            y_all = jnp.einsum('etm,emh->eth', gp * up, w_down)
            y_sel = y_all[topk_idx, jnp.arange(T)[:, None], :]
            y = (y_sel * topk_w[..., None]).sum(1).reshape(b, s, h)
            p = _leaky(hidden_states @ sw_gate) * (hidden_states @ sw_up) @ sw_down
            y = y + p
            num = jnp.sum(y * p, -1)
            den = jnp.maximum(jnp.linalg.norm(y, axis=-1), EPS_COS) * jnp.maximum(jnp.linalg.norm(p, axis=-1), EPS_COS)
            closs = CONS_ALPHA * jnp.mean(num / den / (1.0 + COS_TEMP))
            return (y, aux_loss + closs)
        y, _ = _moe_forward(hidden_states, g, wt, wg, w_gate, w_up, w_down, sw_gate, sw_up, sw_down)
        return y

    def _L1_cond_ref(x, attn_bias, mask, g_in, null_attn_bias, null_kv, Wq, Wkv, Wo, g_out):
        import jax, jax.numpy as jnp
        import numpy as np
        B, N, DIM, H, DH = (2, 256, 128, 16, 64)
        INNER = H * DH
        EPS = 1e-05

        def layernorm(x, g):
            mean = jnp.mean(x, axis=-1, keepdims=True)
            var = jnp.var(x, axis=-1, keepdims=True)
            return (x - mean) * jax.lax.rsqrt(var + EPS) * g
        b, n, _ = x.shape
        scale = DH ** (-0.5)
        xn = layernorm(x, g_in)
        q = (xn @ Wq).reshape(b, n, H, DH).transpose(0, 2, 1, 3) * scale
        kv = xn @ Wkv
        k, v = (kv[..., :DH], kv[..., DH:])
        nk = jnp.broadcast_to(null_kv[0], (b, 1, DH))
        nv = jnp.broadcast_to(null_kv[1], (b, 1, DH))
        k = jnp.concatenate([nk, k], axis=1)
        v = jnp.concatenate([nv, v], axis=1)
        sim = jnp.einsum('bhid,bjd->bhij', q, k)
        null_col = jnp.broadcast_to(null_attn_bias[:, None, None], (H, n, 1))
        bias = jnp.concatenate([null_col, attn_bias], axis=-1)
        sim = sim + bias
        neg = -jnp.finfo(sim.dtype).max
        j = n + 1
        causal_mask = jnp.triu(jnp.ones((n, j), dtype=bool), k=j - n + 1)
        sim = jnp.where(causal_mask, neg, sim)
        mask_p = jnp.pad(mask, ((0, 0), (1, 0)), constant_values=True)
        sim = jnp.where(mask_p[:, None, None, :], sim, neg)
        attn = jax.nn.softmax(sim, axis=-1)
        out = jnp.einsum('bhij,bjd->bhid', attn, v)
        out = out.transpose(0, 2, 1, 3).reshape(b, n, INNER)
        out = out @ Wo
        return layernorm(out, g_out)
    x = x + _L0_cond_ref(x, cond_64, L0_cond_wt, L0_cond_wg, L0_cond_w_gate, L0_cond_w_up, L0_cond_w_down, L0_cond_sw_gate, L0_cond_sw_up, L0_cond_sw_down)
    x = x + _L1_cond_ref(x, fside_16xSxS_0, mask_BxS_bk0, L1_cond_g_in, L1_cond_null_attn_bias, cond_64, L1_cond_Wq, L1_cond_Wkv, L1_cond_Wo, L1_cond_g_out)
    return x

_drawn_inputs = setup_inputs


def setup_inputs(seed=0):
    import zlib

    import numpy as np

    out = dict(_drawn_inputs(seed))
    spreads = {'L1_cond_g_in': (1.0, 0.2), 'L1_cond_g_out': (1.0, 0.2)}
    factors = {}
    for name, (base, spread) in spreads.items():
        noise = np.random.default_rng([zlib.crc32(name.encode()), seed]).standard_normal(out[name].shape)
        drawn = base * np.exp(spread * noise) if base else spread * noise
        out[name] = jnp.asarray(drawn.astype(out[name].dtype))
    for name, factor in factors.items():
        out[name] = (out[name] * factor).astype(out[name].dtype)
    return out
```

```python
import concourse.bass as bass
from concourse import mybir
from contextlib import ExitStack


def moe_then_attention_program(nc, x, cond, score_bias, keep_mask, wt, wg, w_gate, w_up, w_down,
                               sw_gate, sw_up, sw_down, g_in, null_bias, w_q, w_kv, w_o, g_out, out):
    f32, f32r, u8 = mybir.dt.float32, mybir.dt.float32r, mybir.dt.uint8
    bf16 = mybir.dt.bfloat16
    ALU, ACT, AX = mybir.AluOpType, mybir.ActivationFunctionType, mybir.AxisListType

    P = 128
    B, S, C = x.shape
    E, G = wg.shape
    M = w_gate.shape[2]
    H = null_bias.shape[0]
    D = w_kv.shape[1] // 2
    QT = S // P
    U = B * QT
    T = B * S
    PAIRS = H // 2
    EP = E // 2
    NM = EP + 1
    SHARED = EP
    NEG = -1.0e30
    EPS = 1e-5
    SLOPE = 0.01

    GROUPS = [[(0, 3, 0)], [(0, 2, 0), (0, 0, 3 * P)], [(1, 3, 0)], [(1, 2, 0), (1, 0, 3 * P)],
              [(0, 1, 0), (1, 1, 2 * P)]]
    NG = len(GROUPS)
    SLOTS = 2 * NG
    before = [sum(len(GROUPS[j % NG]) for j in range(k)) for k in range(SLOTS + 1)]
    UNITS = before[SLOTS]

    ctx = ExitStack()
    with ctx:
        def sb(name, shape, dt=f32):
            return ctx.enter_context(nc.sbuf_tensor(name, shape, dt))

        def sem(name):
            return ctx.enter_context(nc.semaphore(name))

        x_sb = sb("x_sb", [P, U, C])
        wt_sb = sb("wt_sb", [E, C])
        wg_sb = sb("wg_sb", [E, G])
        cond_sb = sb("cond_sb", [B, G])
        gate_sb = sb("gate_sb", [P, NM, P])
        up_sb = sb("up_sb", [P, NM, P])
        down_sb = sb("down_sb", [P, NM, C])
        wq_sb = sb("wq_sb", [P, PAIRS * P])
        wkv_sb = sb("wkv_sb", [P, 2 * D])
        wo_sb = sb("wo_sb", [P, PAIRS * C])
        g_in_col = sb("g_in_col", [P, 1])
        g_out_row = sb("g_out_row", [P, C])
        null_bias_row = sb("null_bias_row", [P, H])
        null_k_row = sb("null_k_row", [P, D])
        null_v_col = sb("null_v_col", [P, 1])
        keep_row = sb("keep_row", [D + 1, T], u8)
        bias_sb = sb("bias_sb", [P, 2, QT, S])

        ident = sb("ident", [P, P])
        earlier = sb("earlier", [P, E, E])
        pick = sb("pick", [32 + E, EP, P])
        pick_r = sb("pick_r", [32 + E, EP, P], f32r)
        minus_half = sb("minus_half", [P, QT])
        zero_bf = sb("zero_bf", [P, S], bf16)
        place_v = sb("place_v", [P, PAIRS * H])

        xT = sb("xT", [P, T])
        wtT = sb("wtT", [P, E])
        wgT = sb("wgT", [G, E])
        condT = sb("condT", [G, B, P])
        top = sb("top", [P, U])
        logit = sb("logit", [P, U, E])
        expo = sb("expo", [P, U, E])
        total = sb("total", [P, U])
        score = sb("score", [P, U, E])
        greater = sb("greater", [P, U, E * E])
        equal = sb("equal", [P, U, E * E])
        rank = sb("rank", [P, U, E])
        chosen = sb("chosen", [P, U, E])
        weight = sb("weight", [P, U, E])
        weightT = sb("weightT", [32 + E, T], f32r)
        leaky = sb("leaky", [P, 2, S])
        hidden = sb("hidden", [P, NM, T])
        x1 = sb("x1", [P, U, C])

        stats = sb("stats", [P, U, 6])
        moments = sb("moments", [P, U, 2])
        var_eps = sb("var_eps", [P, U])
        rstd = sb("rstd", [P, U])
        xn = sb("xn", [P, U, C])
        xnT_hi = sb("xnT_hi", [P, T], f32r)
        xnT_lo = sb("xnT_lo", [P, T], f32r)

        VW = D + H
        vw = sb("vw", [P, VW])
        null_prod = sb("null_prod", [P, H * D])
        wk_hi = sb("wk_hi", [P, P], f32r)
        wk_lo = sb("wk_lo", [P, P], f32r)
        vw_hi = sb("vw_hi", [P, VW], f32r)
        vw_lo = sb("vw_lo", [P, VW], f32r)
        wq_hi = sb("wq_hi", [P, P], f32r)
        wq_lo = sb("wq_lo", [P, P], f32r)
        k_hi = sb("k_hi", [P, T], f32r)
        k_lo = sb("k_lo", [D + 1, T], f32r)
        v_sb = sb("v_sb", [P, U, D])
        neg_null = sb("neg_null", [P, H, U])
        neg_null_now = sb("neg_null_now", [P, 2, U])

        q_hi = sb("q_hi", [P, T], f32r)
        q_lo = sb("q_lo", [P, T], f32r)
        q_both = [sb(f"q_both{h}", [P, T], f32r) for h in range(2)]
        q_one = [sb(f"q_one{h}", [D + 1, T], f32r) for h in range(2)]

        neg_s = sb("neg_s", [P, 2, S])
        probs = sb("probs", [P, 2, S])
        probsT = sb("probsT", [P, 2, S])
        neg_max = sb("neg_max", [P, 2, U])
        row_sum = sb("row_sum", [P, 2, U])
        null_gap = sb("null_gap", [P, 2, U])
        null_exp = sb("null_exp", [P, 2, U])
        full_sum = sb("full_sum", [P, 2, U])
        inv_sum = sb("inv_sum", [P, 2, U])
        null_prob = sb("null_prob", [P, U, H])
        heads = sb("heads", [P, U, P])
        headsT = sb("headsT", [P, T])
        null_out = sb("null_out", [H, C])
        null_probT = sb("null_probT", [H, T])
        normed = sb("normed", [P, U, C])
        result = sb("result", [P, U, C])

        bank = [ctx.enter_context(nc.psum_tensor(f"bank{i}", [P, S], f32)) for i in range(8)]
        S_BANK, T_BANK, PV_BANK, X_BANK, F_BANK = bank[0:2], bank[2:4], bank[4], bank[5], bank[6:8]
        GATE_BANK, UP_BANK, Y_BANK, W_BANK = bank[0:2], bank[2:4], bank[4:6], bank[6:8]

        ld = {n: sem("ld_" + n) for n in ("x", "router", "gate", "up", "down", "sgate", "sup", "sdown",
                                          "wq", "wkv", "wo", "norm", "null", "null_v", "mask")}
        bias_ld = [sem("bias_ld_a"), sem("bias_ld_b")]
        const_step, ident_ok, consts_ok, zero_ok = (sem(n) for n in ("const_step", "ident_ok", "consts_ok", "zero_ok"))
        vw_step, wkv_split_ok, null_prod_ok, wq_split = (sem(n) for n in ("vw_step", "wkv_split_ok", "null_prod_ok", "wq_split"))
        rstd_ok, null_now_ok, gap_ok, sum_ok, nullp_ok = (sem(n) for n in ("rstd_ok", "null_now_ok", "gap_ok", "sum_ok", "nullp_ok"))
        bias_ok = [sem("bias_ok_a"), sem("bias_ok_b")]
        wq_hi_ok = sem("wq_hi_ok")
        xT_ps, small_ps, logit_ps, gu_ps, wT_ps, wb_ps, y_ps = (sem(n) for n in (
            "xT_ps", "small_ps", "logit_ps", "gu_ps", "wT_ps", "wb_ps", "y_ps"))
        xnT_ps, k_ps, v_ps, fin_zero, q_ps, s_ps, t_ps, pv_ps, hT_ps, wo_ps = (sem(n) for n in (
            "xnT_ps", "k_ps", "v_ps", "fin_zero", "q_ps", "s_ps", "t_ps", "pv_ps", "hT_ps", "wo_ps"))
        nout_ps, npT_ps, fin_ps = (sem(n) for n in ("nout_ps", "npT_ps", "fin_ps"))
        xT_a, expo_ok, sloped_ok, wTh_ok, xnTh_ok, kh_ok, exp_ok, evac_a, qhi_ok, nexp_ok, hT_ok, npT_a = (sem(n) for n in (
            "xT_a", "expo_ok", "sloped_ok", "wTh_ok", "xnTh_ok", "kh_ok", "exp_ok", "evac_a", "qhi_ok",
            "nexp_ok", "hT_ok", "npT_a"))
        xT_v, small_ok, dve_step, logit_ok, weight_ok, t1_ok, h_ok, wTl_ok, x1_ok, var_ok, xn_ok, xnTl_ok = (sem(n) for n in (
            "xT_v", "small_ok", "dve_step", "logit_ok", "weight_ok", "t1_ok", "h_ok", "wTl_ok", "x1_ok",
            "var_ok", "xn_ok", "xnTl_ok"))
        wn_ok, kl_ok, v_ok, negnull_ok, mask_ok, place_ok, leaky_ok, neg_ok, evac_v, qlo_ok, inv_ok, head_ok = (sem(n) for n in (
            "wn_ok", "kl_ok", "v_ok", "negnull_ok", "mask_ok", "place_ok", "leaky_ok", "neg_ok", "evac_v", "qlo_ok",
            "inv_ok", "head_ok"))
        nout_ok, npT_v, result_ok = (sem(n) for n in ("nout_ok", "npT_v", "result_ok"))
        q_ok = [sem("q_ok_a"), sem("q_ok_b")]
        stored = sem("stored")
        dve_passed, pool_passed = sem("dve_passed"), sem("pool_passed")

        tiles = lambda a: a.rearrange("b (t p) c -> p (b t) c", p=P)
        bias_view = score_bias.rearrange("h (t p) j -> p h t j", p=P)
        cols = lambda u: slice(u * P, (u + 1) * P)
        half = lambda n: slice(n * S, (n + 1) * S)

        STEPS = [(SHARED, 0), (SHARED, 1)] + [(m, n) for n in range(B) for m in range(EP)]

        def stand_alone(engine, passed):
            engine.sem_inc(passed, 1)

        def loop(engine, body):
            body(0, True, False)
            with engine.Fori(1, PAIRS - 1) as p:
                body(p, False, False)
            body(PAIRS - 1, False, True)

        block = ctx.enter_context(nc.Block())

        @block.sync
        def _(sp):
            sp.dma_start(x_sb[:], tiles(x)).then_inc(ld["x"], 16)
            sp.dma_start(wt_sb[:], wt).then_inc(ld["router"], 16)
            sp.dma_start(wg_sb[:], wg).then_inc(ld["router"], 16)
            sp.dma_start(cond_sb[:], cond).then_inc(ld["router"], 16)
            sp.dma_start(gate_sb[:, SHARED, :], sw_gate).then_inc(ld["sgate"], 16)
            sp.dma_start(up_sb[:, SHARED, :], sw_up).then_inc(ld["sup"], 16)
            sp.dma_start(gate_sb[:, 0:EP, :].rearrange("c e (k m) -> c (e k) m", k=2),
                         w_gate.rearrange("e c m -> c e m")).then_inc(ld["gate"], 16)
            sp.dma_start(up_sb[:, 0:EP, :].rearrange("c e (k m) -> c (e k) m", k=2),
                         w_up.rearrange("e c m -> c e m")).then_inc(ld["up"], 16)
            sp.dma_start(wkv_sb[:], w_kv).then_inc(ld["wkv"], 16)
            sp.dma_start(wq_sb[:], w_q).then_inc(ld["wq"], 16)
            sp.dma_start(null_k_row[:], cond[0:1, :].broadcast_to([P, D])).then_inc(ld["null"], 16)
            sp.dma_start(null_bias_row[:], null_bias.rearrange("(a h) -> a h", a=1).broadcast_to([P, H])).then_inc(ld["null"], 16)
            sp.dma_start(down_sb[:, SHARED, :], sw_down).then_inc(ld["sdown"], 16)
            sp.dma_start(down_sb[:, 0:EP, :], w_down.rearrange("(e k) m c -> (k m) e c", k=2)).then_inc(ld["down"], 16)
            sp.dma_start(keep_row[D:D + 1, :], keep_mask.rearrange("(a b) s -> a (b s)", a=1)).then_inc(ld["mask"], 16)
            sp.dma_start(g_in_col[:], g_in.rearrange("(c a) -> c a", a=1)).then_inc(ld["norm"], 16)
            sp.dma_start(g_out_row[:], g_out.rearrange("(a c) -> a c", a=1).broadcast_to([P, C])).then_inc(ld["norm"], 16)
            for k in range(2):
                sp.dma_start(null_v_col[k * D:(k + 1) * D, :], cond[1:2, :].rearrange("a d -> d a")).then_inc(ld["null_v"], 16)

            def load_bias(h, which):
                for t in range(QT):
                    sp.dma_start(bias_sb[:, which:which + 1, t, 0:(t + 1) * P],
                                 bias_view[:, bass.ds(h, 1), t, 0:(t + 1) * P]).then_inc(bias_ld[which], 16)

            def copy_queries(which):
                own = slice(which * D, (which + 1) * D)
                sp.dma_start(q_both[which][0:D, :].bitcast(f32), q_hi[own, :].bitcast(f32)).then_inc(q_ok[which], 16)
                sp.dma_start(q_both[which][D:P, :].bitcast(f32), q_lo[own, :].bitcast(f32)).then_inc(q_ok[which], 16)
                sp.dma_start(q_one[which][0:D, :].bitcast(f32), q_hi[own, :].bitcast(f32)).then_inc(q_ok[which], 16)

            load_bias(0, 0)
            load_bias(1, 1)
            sp.dma_start(wo_sb[:].rearrange("p (a c) -> p a c", c=C), w_o.rearrange("(a p) c -> p a c", p=P)).then_inc(ld["wo"], 16)
            sp.wait_ge(qhi_ok, B)
            sp.wait_ge(qlo_ok, B)
            copy_queries(0)
            copy_queries(1)

            def body(p, first, last):
                if last:
                    return
                sp.wait_ge(qhi_ok, B * p + 2 * B)
                sp.wait_ge(qlo_ok, B * p + 2 * B)
                sp.wait_ge(s_ps, SLOTS * p + NG)
                copy_queries(0)
                sp.wait_ge(neg_ok, UNITS * p + before[NG])
                load_bias(2 * p + 2, 0)
                sp.wait_ge(s_ps, SLOTS * p + SLOTS)
                copy_queries(1)
                sp.wait_ge(neg_ok, UNITS * p + UNITS)
                load_bias(2 * p + 3, 1)

            loop(nc.sync, body)
            for n in range(B):
                sp.wait_ge(result_ok, n + 1)
                sp.dma_start(tiles(out)[:, n * QT:(n + 1) * QT, :], result[:, n * QT:(n + 1) * QT, :]).then_inc(stored, 16)
            sp.wait_ge(stored, 16 * B)

        @block.gpsimd
        def _(pool):
            steps = [0]

            def step(ins):
                steps[0] += 1
                ins.then_inc(const_step, 1)
                pool.wait_ge(const_step, steps[0])

            step(pool.memset(ident[:], 0.0))
            pool.affine_select(out=ident[:], in_=ident[:], compare_op=ALU.not_equal, fill=1.0, base=0,
                               pattern=[[-1, P]], channel_multiplier=1).then_inc(ident_ok, 1)
            step(pool.memset(earlier[:], 1.0))
            step(pool.affine_select(out=earlier[:], in_=earlier[:], compare_op=ALU.is_gt, fill=0.0, base=0,
                                    pattern=[[1, E], [-1, E]], channel_multiplier=0))
            step(pool.memset(pick[:], 0.0))
            for base in (0, -32):
                step(pool.affine_select(out=pick[:], in_=pick[:], compare_op=ALU.not_equal, fill=1.0, base=base,
                                        pattern=[[-2, EP], [-1, 2], [0, M]], channel_multiplier=1))
            step(pool.tensor_copy(pick_r[:], pick[:]))
            step(pool.memset(minus_half[:], -0.5))
            for h in range(2):
                step(pool.memset(q_one[h][D:D + 1, :].bitcast(f32), 1.0))
            pool.memset(zero_bf[:], 0.0).then_inc(zero_ok, 1)
            pool.memset(place_v[:], 0.0).then_inc(consts_ok, 1)

            pool.wait_ge(ld["wkv"], 16)
            for k in range(2):
                pool.tensor_copy(wk_hi[:, k * D:(k + 1) * D], wkv_sb[:, 0:D]).then_inc(vw_step, 1)
            pool.wait_ge(vw_step, 2)
            for k in range(2):
                pool.tensor_tensor(wk_lo[:, k * D:(k + 1) * D], wkv_sb[:, 0:D],
                                   wk_hi[:, k * D:(k + 1) * D].bitcast(f32), ALU.subtract).then_inc(wkv_split_ok, 1)
            pool.wait_ge(ld["wq"], 16)
            pool.wait_ge(ld["null"], 32)
            pool.tensor_tensor(null_prod[:].rearrange("p (h d) -> p h d", d=D), wq_sb[:].rearrange("p (h d) -> p h d", d=D),
                               null_k_row[:].unsqueeze(1).broadcast_to([P, H, D]), ALU.mult).then_inc(null_prod_ok, 1)
            pool.tensor_copy(vw[:, 0:D], wkv_sb[:, D:2 * D]).then_inc(vw_step, 1)
            pool.wait_ge(wn_ok, 1)
            pool.wait_ge(vw_step, 3)
            pool.tensor_copy(vw_hi[:], vw[:]).then_inc(vw_step, 1)
            pool.wait_ge(vw_step, 4)
            pool.tensor_tensor(vw_lo[:], vw[:], vw_hi[:].bitcast(f32), ALU.subtract).then_inc(wkv_split_ok, 1)

            def split_wq(p):
                own = wq_sb[:, bass.ds(p * P, P)]
                pool.tensor_copy(wq_hi[:], own).then_inc(wq_hi_ok, 1)
                pool.wait_ge(wq_hi_ok, p + 1)
                stand_alone(pool, pool_passed)
                pool.tensor_tensor(wq_lo[:], own, wq_hi[:].bitcast(f32), ALU.subtract).then_inc(wq_split, 1)

            def causal(which, done):
                pool.wait_ge(bias_ld[which], 16 * QT * done)
                stand_alone(pool, pool_passed)
                diagonal = bias_sb[:, which, :, :].rearrange("p t j -> p (t j)")
                step_t = S + P
                for t in range(QT):
                    blockd = diagonal[:, t * step_t:t * step_t + P]
                    ins = pool.affine_select(out=blockd, in_=blockd, compare_op=ALU.is_ge, fill=NEG, base=0,
                                             pattern=[[-1, P]], channel_multiplier=1)
                    ins.then_inc(bias_ok[which], 1)

            split_wq(0)

            def rstd_of(n):
                pool.wait_ge(var_ok, n + 1)
                own = slice((n % B) * QT, (n % B + 1) * QT)
                pool.tensor_tensor(rstd[:, own], var_eps[:, own], minus_half[:], ALU.pow).then_inc(rstd_ok, 1)

            rstd_of(0)
            causal(0, 1)
            causal(1, 1)
            rstd_of(1)
            pool.wait_ge(negnull_ok, B)
            for which in range(2):
                pool.tensor_copy(neg_null_now[:, which, :], neg_null[:, which, :]).then_inc(null_now_ok, 1)
            pool.wait_ge(q_ps, B)
            split_wq(1)

            def body(p, first, last):
                if not last:
                    pool.wait_ge(q_ps, B * p + 2 * B)
                    if not isinstance(p, int) or p + 2 < PAIRS:
                        split_wq_next(p)
                for which in range(2):
                    pool.wait_ge(neg_ok, UNITS * p + before[NG * (which + 1)])
                    pool.tensor_tensor(null_gap[:, which, :], neg_max[:, which, :], neg_null_now[:, which, :],
                                       ALU.subtract).then_inc(gap_ok, 1)
                    if not last:
                        pool.wait_ge(gap_ok, 2 * p + which + 1)
                        pool.tensor_copy(neg_null_now[:, which:which + 1, :],
                                         neg_null[:, bass.ds(2 * p + 2 + which, 1), :]).then_inc(null_now_ok, 1)
                    pool.wait_ge(nexp_ok, 2 * p + which + 1)
                    pool.tensor_tensor(full_sum[:, which, :], row_sum[:, which, :], null_exp[:, which, :],
                                       ALU.add).then_inc(sum_ok, 1)
                    pool.wait_ge(inv_ok, 2 * p + which + 1)
                    stand_alone(pool, pool_passed)
                    pool.tensor_tensor(null_prob[:, :, bass.ds(2 * p + which, 1)], null_exp[:, which, :].unsqueeze(2),
                                       inv_sum[:, which, :].unsqueeze(2), ALU.mult).then_inc(nullp_ok, 1)
                    if not last:
                        causal(which, p + 2)

            def split_wq_next(p):
                split_wq(p + 2)

            body(0, True, False)
            with nc.gpsimd.Fori(1, PAIRS - 2) as p:
                body(p, False, False)
            body(PAIRS - 2, False, False)
            body(PAIRS - 1, False, True)
            rstd_of(2)
            rstd_of(3)

        @block.scalar
        def _(act):
            act.wait_ge(xT_ps, 1)
            nc.scalar.activation(xT[:, half(0)], bank[0][:], ACT.Copy).then_inc(xT_a, 1)
            act.wait_ge(logit_ok, 1)
            nc.scalar.activation(expo[:], logit[:], ACT.Exp, scale=0.5).then_inc(expo_ok, 1)

            def leaky_step(s):
                act.wait_ge(gu_ps, s + 1)
                if s >= 2:
                    act.wait_ge(t1_ok, s - 1)
                nc.scalar.activation(leaky[:, s % 2, :], GATE_BANK[s % 2][:], ACT.Copy, scale=SLOPE).then_inc(sloped_ok, 1)

            for s in range(len(STEPS)):
                if s == 4:
                    for n in range(B):
                        act.wait_ge(wT_ps, n + 1)
                        nc.scalar.activation(weightT[0:E, half(n)], W_BANK[n][0:E, :], ACT.Copy).then_inc(wTh_ok, 1)
                leaky_step(s)

            def q_hi_part(b, done, psum):
                act.wait_ge(q_ps, done + 1)
                nc.scalar.activation(q_hi[:, half(b)], psum[:], ACT.Copy, scale=float(D) ** -0.5).then_inc(qhi_ok, 1)

            for n in range(B):
                act.wait_ge(xnT_ps, n + 1)
                if n == 0:
                    act.wait_ge(ld["norm"], 32)
                nc.scalar.activation(xnT_hi[:, half(n)], Y_BANK[n][:], ACT.Copy, scale=g_in_col[:, 0:1]).then_inc(xnTh_ok, 1)
                act.wait_ge(k_ps, n + 1)
                nc.scalar.activation(k_hi[:, half(n)], S_BANK[n][:], ACT.Copy).then_inc(kh_ok, 1)
                q_hi_part(n, n, F_BANK[n])

            def exp_group(p, k):
                which, par = k // NG, k % 2
                at = 0
                for b, t, off in GROUPS[k % NG]:
                    w = (t + 1) * P
                    at += 1
                    act.wait_ge(neg_ok, UNITS * p + before[k] + at)
                    if at == 1 and (not isinstance(p, int) or SLOTS * p + k >= 2):
                        act.wait_ge(t_ps, SLOTS * p + k - 1)
                    u = b * QT + t
                    nc.scalar.activation(probs[:, par, off:off + w], neg_s[:, par, off:off + w], ACT.Exp,
                                         bias=neg_max[:, which, u:u + 1], scale=-1.0,
                                         accum_out=row_sum[:, which, u:u + 1]).then_inc(exp_ok, 1)

            def evac_group(p, k):
                act.wait_ge(t_ps, SLOTS * p + k + 1)
                if not isinstance(p, int) or SLOTS * p + k >= 2:
                    act.wait_ge(pv_ps, SLOTS * p + k - 1)
                nc.scalar.activation(probsT[:, k % 2, :], T_BANK[k % 2][:], ACT.Copy).then_inc(evac_a, 1)

            def null_exp_of(p, which):
                act.wait_ge(gap_ok, 2 * p + which + 1)
                nc.scalar.activation(null_exp[:, which, :], null_gap[:, which, :], ACT.Exp).then_inc(nexp_ok, 1)

            def heads_evac(pair, n):
                act.wait_ge(hT_ps, B * pair + n + 1)
                nc.scalar.activation(headsT[:, half(n)], X_BANK[:], ACT.Copy).then_inc(hT_ok, 1)

            exp_group(0, 0)

            def body(p, first, last):
                for k in range(SLOTS):
                    if k % 2 == 0:
                        evac_group(p, k)
                    if k in (5, 6) and not first:
                        heads_evac(p - 1, k - 5)
                    if k + 1 < SLOTS:
                        exp_group(p, k + 1)
                    elif not last:
                        exp_group(p + 1, 0)
                    if k in (0, 2) and not last:
                        if k == 0:
                            act.wait_ge(q_ok[1], 48 * p + 48)
                        q_hi_part(k // 2, B * p + B + k // 2, X_BANK)
                    if k in (4, 9):
                        null_exp_of(p, k // NG)

            loop(nc.scalar, body)
            for n in range(B):
                heads_evac(PAIRS - 1, n)
            act.wait_ge(npT_ps, 1)
            nc.scalar.activation(null_probT[:, half(0)], bank[0][0:H, :], ACT.Copy).then_inc(npT_a, 1)

        @block.vector
        def _(dve):
            steps = [0]

            def step(ins):
                steps[0] += 1
                ins.then_inc(dve_step, 1)
                dve.wait_ge(dve_step, steps[0])

            nc.vector.memset(weightT[:].bitcast(f32), 0.0).then_inc(dve_step, 1)
            steps[0] += 1
            dve.wait_ge(xT_ps, 2)
            nc.vector.tensor_copy(xT[:, half(1)], bank[1][:]).then_inc(xT_v, 1)
            dve.wait_ge(small_ps, 1)
            nc.vector.tensor_copy(wtT[:], bank[2][:, 0:E])
            nc.vector.tensor_copy(wgT[:], bank[2][0:G, E:2 * E])
            nc.vector.tensor_copy(condT[:], bank[2][0:G, 2 * E:2 * E + B].unsqueeze(2).broadcast_to([G, B, P])).then_inc(small_ok, 1)

            dve.wait_ge(logit_ps, 1)
            logits = Y_BANK[1][:, 0:U * E].rearrange("p (u e) -> p u e", e=E)
            wide = lambda a: a.unsqueeze(2).broadcast_to([P, U, E])
            step(nc.vector.reduce_max(top[:], logits, AX.X))
            nc.vector.tensor_tensor(logit[:], logits, wide(top[:]), ALU.subtract).then_inc(logit_ok, 1)

            def t1_step(s):
                m, n = STEPS[s]
                dve.wait_ge(sloped_ok, s + 1)
                nc.vector.tensor_tensor(leaky[:, s % 2, :], leaky[:, s % 2, :], GATE_BANK[s % 2][:], ALU.max).then_inc(leaky_ok, 1)
                dve.wait_ge(leaky_ok, s + 1)
                ins = nc.vector.tensor_tensor(hidden[:, m, half(n)], leaky[:, s % 2, :], UP_BANK[s % 2][:], ALU.mult)
                ins.then_inc(t1_ok, 1)

            t1_step(0)
            dve.wait_ge(expo_ok, 1)
            step(nc.vector.reduce_sum(total[:], expo[:], AX.X))
            step(nc.vector.reciprocal(total[:], total[:]))
            step(nc.vector.tensor_tensor(score[:], expo[:], wide(total[:]), ALU.mult))
            other = lambda a: a.unsqueeze(2).broadcast_to([P, U, E, E])
            own = lambda a: a.unsqueeze(3).broadcast_to([P, U, E, E])
            four = lambda a: a.rearrange("p u (e f) -> p u e f", f=E)
            nc.vector.tensor_tensor(four(greater[:]), other(score[:]), own(score[:]), ALU.is_gt)
            step(nc.vector.tensor_tensor(four(equal[:]), other(score[:]), own(score[:]), ALU.is_equal))
            dve.wait_ge(consts_ok, 1)
            step(nc.vector.tensor_tensor(equal[:], equal[:], earlier[:].rearrange("p e f -> p (e f)").unsqueeze(1)
                                         .broadcast_to([P, U, E * E]), ALU.mult))
            t1_step(1)
            step(nc.vector.tensor_tensor(equal[:], equal[:], greater[:], ALU.add))
            step(nc.vector.reduce_sum(rank[:], four(equal[:]), AX.X))
            step(nc.vector.scalar_tensor_tensor(out=chosen[:], in0=rank[:], scalar=1.5, in1=score[:],
                                                op0=ALU.is_lt, op1=ALU.mult))
            step(nc.vector.reduce_sum(total[:], chosen[:], AX.X))
            step(nc.vector.tensor_scalar_add(total[:], total[:], 1e-20))
            step(nc.vector.reciprocal(total[:], total[:]))
            nc.vector.tensor_tensor(weight[:], chosen[:], wide(total[:]), ALU.mult).then_inc(weight_ok, 1)
            t1_step(2)
            for n in range(B):
                dve.wait_ge(wTh_ok, n + 1)
                nc.vector.tensor_tensor(weightT[32:32 + E, half(n)], W_BANK[n][0:E, :],
                                        weightT[0:E, half(n)].bitcast(f32), ALU.subtract).then_inc(wTl_ok, 1)

            def h_step(s):
                m, n = STEPS[s]
                dve.wait_ge(wb_ps, s - 1)
                dve.wait_ge(t1_ok, s + 1)
                nc.vector.tensor_tensor(hidden[:, m, half(n)], hidden[:, m, half(n)], W_BANK[s % 2][:], ALU.mult).then_inc(h_ok, 1)

            def norm_tokens(n):
                own = slice(n * QT, (n + 1) * QT)
                dve.wait_ge(y_ps, n + 1)
                nc.vector.tensor_tensor(x1[:, own, :], x_sb[:, own, :], Y_BANK[n][:].rearrange("p (u c) -> p u c", c=C),
                                        ALU.add).then_inc(x1_ok, 1)
                dve.wait_ge(x1_ok, n + 1)
                for u in range(n * QT, (n + 1) * QT):
                    last = nc.vector.bn_stats(stats[:, u, :], x1[:, u, :])
                step(last)
                for u in range(n * QT, (n + 1) * QT):
                    last = nc.vector.bn_aggr(moments[:, u, :], stats[:, u, :])
                step(last)
                nc.vector.tensor_scalar_add(var_eps[:, own], moments[:, own, 1], EPS).then_inc(var_ok, 1)

            def scale_tokens(n):
                dve.wait_ge(rstd_ok, n + 1)
                for u in range(n * QT, (n + 1) * QT):
                    last = nc.vector.tensor_scalar(xn[:, u, :], x1[:, u, :], moments[:, u, 0:1], rstd[:, u:u + 1],
                                                   ALU.subtract, ALU.mult)
                last.then_inc(xn_ok, 1)

            def q_lo_part(b, done, psum):
                dve.wait_ge(qhi_ok, done + 1)
                nc.vector.scalar_tensor_tensor(out=q_lo[:, half(b)], in0=psum[:], scalar=float(D) ** -0.5,
                                               in1=q_hi[:, half(b)].bitcast(f32), op0=ALU.mult,
                                               op1=ALU.subtract).then_inc(qlo_ok, 1)

            for s in range(2, len(STEPS)):
                if s > 2:
                    t1_step(s)
                h_step(s)
                if s == 3:
                    dve.wait_ge(null_prod_ok, 1)
                    nc.vector.reduce_sum(vw[:, D:VW], null_prod[:].rearrange("p (h d) -> p h d", d=D), AX.X).then_inc(wn_ok, 1)
                if s == 4:
                    dve.wait_ge(ld["mask"], 16)
                    nc.vector.tensor_scalar(k_lo[D:D + 1, :], keep_row[D:D + 1, :], -NEG, NEG, ALU.mult, ALU.add).then_inc(mask_ok, 1)
                    dve.wait_ge(ld["null_v"], 32)
                    for k in range(2):
                        nc.vector.tensor_copy(place_v[k * D:(k + 1) * D, k::H + 2],
                                              null_v_col[k * D:(k + 1) * D, 0:1].broadcast_to([D, PAIRS])).then_inc(place_ok, 1)
                if s == 7:
                    norm_tokens(0)
                if s == 8:
                    scale_tokens(0)
            def keys_values(n):
                dve.wait_ge(xnTh_ok, n + 1)
                nc.vector.scalar_tensor_tensor(out=xnT_lo[:, half(n)], in0=Y_BANK[n][:], scalar=g_in_col[:, 0:1],
                                               in1=xnT_hi[:, half(n)].bitcast(f32), op0=ALU.mult,
                                               op1=ALU.subtract).then_inc(xnTl_ok, 1)

            def keys_lo(n):
                dve.wait_ge(kh_ok, n + 1)
                nc.vector.tensor_tensor(k_lo[0:D, half(n)], S_BANK[n][0:D, :], k_hi[0:D, half(n)].bitcast(f32),
                                        ALU.subtract).then_inc(kl_ok, 1)
                dve.wait_ge(v_ps, n + 1)
                made = T_BANK[n][:, 0:QT * VW].rearrange("p (u w) -> p u w", w=VW)
                nc.vector.tensor_copy(v_sb[:, n * QT:(n + 1) * QT, :], made[:, :, 0:D]).then_inc(v_ok, 1)
                nc.vector.scalar_tensor_tensor(
                    out=neg_null[:, :, n * QT:(n + 1) * QT].rearrange("p h u -> p u h"), in0=made[:, :, D:VW],
                    scalar=-float(D) ** -0.5, in1=null_bias_row[:].unsqueeze(1).broadcast_to([P, QT, H]),
                    op0=ALU.mult, op1=ALU.subtract).then_inc(negnull_ok, 1)
                q_lo_part(n, n, F_BANK[n])

            keys_values(0)
            norm_tokens(1)
            keys_lo(0)
            scale_tokens(1)
            keys_values(1)
            keys_lo(1)

            def score_group(p, k):
                which, par = k // NG, k % 2
                dve.wait_ge(s_ps, SLOTS * p + k + 1)
                if not isinstance(p, int) or SLOTS * p + k >= 2:
                    dve.wait_ge(exp_ok, UNITS * p + before[k] - (len(GROUPS[(k - 1) % NG])))
                if k % NG == 0:
                    dve.wait_ge(bias_ok[which], QT * p + QT)
                    dve.wait_ge(null_now_ok, 2 * p + which + 1)
                stand_alone(dve, dve_passed)
                for b, t, off in GROUPS[k % NG]:
                    w = (t + 1) * P
                    u = b * QT + t
                    nc.vector.tensor_tensor_reduce(
                        out=neg_s[:, par, off:off + w], in0=S_BANK[par][:, off:off + w], in1=bias_sb[:, which, t, 0:w],
                        scale=-1.0, scalar=neg_null_now[:, which, u:u + 1], op0=ALU.add, op1=ALU.min,
                        accum_out=neg_max[:, which, u:u + 1]).then_inc(neg_ok, 1)

            def evac_group(p, k):
                dve.wait_ge(t_ps, SLOTS * p + k + 1)
                if not isinstance(p, int) or SLOTS * p + k >= 2:
                    dve.wait_ge(pv_ps, SLOTS * p + k - 1)
                nc.vector.tensor_copy(probsT[:, k % 2, :], T_BANK[k % 2][:]).then_inc(evac_v, 1)

            def invert(p, which):
                dve.wait_ge(sum_ok, 2 * p + which + 1)
                nc.vector.reciprocal(inv_sum[:, which, :], full_sum[:, which, :]).then_inc(inv_ok, 1)

            def normalise(p, which):
                dve.wait_ge(inv_ok, 2 * p + which + 1)
                dve.wait_ge(pv_ps, SLOTS * p + NG * (which + 1))
                nc.vector.tensor_tensor(heads[:, :, which * D:(which + 1) * D], PV_BANK[:].rearrange("p (u d) -> p u d", d=D),
                                        inv_sum[:, which, :].unsqueeze(2).broadcast_to([P, U, D]), ALU.mult).then_inc(head_ok, 1)

            score_group(0, 0)

            def body(p, first, last):
                for k in range(SLOTS):
                    if k == 0 and not first:
                        invert(p - 1, 1)
                    if k == 1 and not first:
                        normalise(p - 1, 1)
                    if k == 5:
                        invert(p, 0)
                    if k == 6:
                        if not first:
                            dve.wait_ge(hT_ps, B * p)
                        normalise(p, 0)
                    if k + 1 < SLOTS:
                        score_group(p, k + 1)
                    elif not last:
                        score_group(p + 1, 0)
                    if k in (0, 3) and not last:
                        q_lo_part(k // 3, B * p + B + k // 3, X_BANK)
                    if k % 2 == 1:
                        evac_group(p, k)

            loop(nc.vector, body)
            invert(PAIRS - 1, 1)
            normalise(PAIRS - 1, 1)
            dve.wait_ge(nout_ps, 1)
            nc.vector.tensor_copy(null_out[:], PV_BANK[0:H, 0:C]).then_inc(nout_ok, 1)
            dve.wait_ge(npT_ps, 2)
            nc.vector.tensor_copy(null_probT[:, half(1)], bank[1][0:H, :]).then_inc(npT_v, 1)
            for n in range(B):
                own = slice(n * QT, (n + 1) * QT)
                dve.wait_ge(fin_ps, n + 1)
                for u in range(QT):
                    last = nc.vector.bn_stats(stats[:, n * QT + u, :], F_BANK[n][:, cols(u)])
                step(last)
                for u in range(n * QT, (n + 1) * QT):
                    last = nc.vector.bn_aggr(moments[:, u, :], stats[:, u, :])
                step(last)
                nc.vector.tensor_scalar_add(var_eps[:, own], moments[:, own, 1], EPS).then_inc(var_ok, 1)
            for n in range(B):
                own = slice(n * QT, (n + 1) * QT)
                dve.wait_ge(rstd_ok, B + n + 1)
                for u in range(n * QT, (n + 1) * QT):
                    last = nc.vector.tensor_scalar(normed[:, u, :], F_BANK[n][:, cols(u % QT)], moments[:, u, 0:1],
                                                   rstd[:, u:u + 1], ALU.subtract, ALU.mult)
                step(last)
                step(nc.vector.tensor_tensor(result[:, own, :], normed[:, own, :],
                                             g_out_row[:].unsqueeze(1).broadcast_to([P, QT, C]), ALU.mult))
                nc.vector.tensor_tensor(result[:, own, :], result[:, own, :], x1[:, own, :], ALU.add).then_inc(result_ok, 1)

        @block.tensor
        def _(pe):
            def mm(o, a, b, start=True, stop=True, loose=False):
                return nc.tensor.matmul(o, a, b, start=start, stop=stop, skip_group_check=loose)

            def three(o, a_hi, a_lo, b_hi, b_lo):
                mm(o, a_hi, b_hi, True, False)
                mm(o, a_lo, b_hi, False, False)
                return mm(o, a_hi, b_lo, False, True)

            pe.wait_ge(ident_ok, 1)
            pe.wait_ge(ld["x"], 16)
            for n in range(B):
                for u in range(QT):
                    last = nc.tensor.transpose(bank[n][:, cols(u)], x_sb[:, n * QT + u, :], ident[:])
                last.then_inc(xT_ps, 1)
            pe.wait_ge(ld["router"], 48)
            nc.tensor.transpose(bank[2][:, 0:E], wt_sb[:], ident[0:E, 0:E])
            nc.tensor.transpose(bank[2][0:G, E:2 * E], wg_sb[:], ident[0:E, 0:E])
            nc.tensor.transpose(bank[2][0:G, 2 * E:2 * E + B], cond_sb[:], ident[0:B, 0:B]).then_inc(small_ps, 1)
            pe.wait_ge(small_ok, 1)
            pe.wait_ge(xT_a, 1)
            pe.wait_ge(xT_v, 1)
            for u in range(U):
                mm(Y_BANK[1][:, u * E:(u + 1) * E], xT[:, cols(u)], wtT[:], True, False)
                last = mm(Y_BANK[1][:, u * E:(u + 1) * E], condT[:, u // QT, :], wgT[:], False, True)
            last.then_inc(logit_ps, 1)

            def gate_up(s):
                m, n = STEPS[s]
                if s == 0:
                    pe.wait_ge(ld["sgate"], 16)
                    pe.wait_ge(ld["sup"], 16)
                if s == 2:
                    pe.wait_ge(ld["gate"], 16)
                    pe.wait_ge(ld["up"], 16)
                if s >= 2:
                    pe.wait_ge(t1_ok, s - 1)
                mm(GATE_BANK[s % 2][:], gate_sb[:, m, :], xT[:, half(n)])
                mm(UP_BANK[s % 2][:], up_sb[:, m, :], xT[:, half(n)]).then_inc(gu_ps, 1)

            def weights_wide(s):
                m, n = STEPS[s]
                pe.wait_ge(wTl_ok, B)
                if s >= 4:
                    pe.wait_ge(h_ok, s - 3)
                mm(W_BANK[s % 2][:], pick_r[:, m, :], weightT[:, half(n)]).then_inc(wb_ps, 1)

            def down(n):
                pe.wait_ge(h_ok, EP * (n + 1))
                if n == 0:
                    pe.wait_ge(ld["down"], 16)
                    pe.wait_ge(ld["sdown"], 16)
                for u in range(QT):
                    for m in range(NM):
                        last = mm(Y_BANK[n][:, cols(u)], hidden[:, m, cols(n * QT + u)], down_sb[:, m, :], m == 0, m == NM - 1)
                last.then_inc(y_ps, 1)

            def tokensT(n):
                pe.wait_ge(xn_ok, n + 1)
                for u in range(QT):
                    last = nc.tensor.transpose(Y_BANK[n][:, cols(u)], xn[:, n * QT + u, :], ident[:])
                last.then_inc(xnT_ps, 1)

            def queries(b, psum):
                three(psum[:], wq_hi[:], wq_lo[:], xnT_hi[:, half(b)], xnT_lo[:, half(b)]).then_inc(q_ps, 1)

            def keys_values(n):
                pe.wait_ge(xnTl_ok, n + 1)
                if n == 0:
                    pe.wait_ge(wkv_split_ok, 3)
                    pe.wait_ge(wq_split, 1)
                three(S_BANK[n][:], wk_hi[:], wk_lo[:], xnT_hi[:, half(n)], xnT_lo[:, half(n)]).then_inc(k_ps, 1)
                for u in range(QT):
                    own = cols(n * QT + u)
                    o = T_BANK[n][:, u * VW:(u + 1) * VW]
                    last = three(o, xnT_hi[:, own], xnT_lo[:, own], vw_hi[:], vw_lo[:])
                last.then_inc(v_ps, 1)
                queries(n, F_BANK[n])

            for s in range(4):
                gate_up(s)
            pe.wait_ge(weight_ok, 1)
            for n in range(B):
                for u in range(QT):
                    last = nc.tensor.transpose(W_BANK[n][0:E, cols(u)], weight[:, n * QT + u, :], ident[:])
                last.then_inc(wT_ps, 1)
            weights_wide(2)
            weights_wide(3)
            for s in range(4, len(STEPS)):
                gate_up(s)
                weights_wide(s)
                if s == 6:
                    down(0)
            tokensT(0)
            down(1)
            pe.wait_ge(h_ok, len(STEPS) - 2)
            keys_values(0)
            tokensT(1)
            keys_values(1)
            pe.wait_ge(qlo_ok, B)
            pe.wait_ge(zero_ok, 1)
            for n in range(B):
                mm(F_BANK[n][:], zero_bf[:, 0:P], zero_bf[:], True, False, loose=True).then_inc(fin_zero, 1)

            def scores(p, k):
                which = k // NG
                if k % NG == 0:
                    pe.wait_ge(q_ok[which], 48 * p + 48)
                if not isinstance(p, int) or SLOTS * p + k >= 2:
                    pe.wait_ge(neg_ok, UNITS * p + before[k] - len(GROUPS[(k - 1) % NG]))
                for b, t, off in GROUPS[k % NG]:
                    w = (t + 1) * P
                    keys = slice(b * S, b * S + w)
                    mm(S_BANK[k % 2][:, off:off + w], q_both[which][:, cols(b * QT + t)], k_hi[:, keys], True, False)
                    last = mm(S_BANK[k % 2][:, off:off + w], q_one[which][:, cols(b * QT + t)], k_lo[:, keys], False, True)
                last.then_inc(s_ps, 1)

            def transposes(p, k):
                pe.wait_ge(exp_ok, UNITS * p + before[k + 1])
                if not isinstance(p, int) or SLOTS * p + k >= 2:
                    pe.wait_ge(evac_a if k % 2 == 0 else evac_v, NG * p + k // 2)
                for j in range(QT):
                    last = nc.tensor.transpose(T_BANK[k % 2][:, cols(j)], probs[:, k % 2, cols(j)], ident[:])
                last.then_inc(t_ps, 1)

            def values(p, k):
                pe.wait_ge(evac_a if k % 2 == 0 else evac_v, NG * p + k // 2 + 1)
                if k % NG == 0 and (not isinstance(p, int) or 2 * p + k // NG > 0):
                    pe.wait_ge(head_ok, 2 * p + k // NG)
                for b, t, off in GROUPS[k % NG]:
                    u = b * QT + t
                    for j in range(t + 1):
                        last = mm(PV_BANK[:, u * D:(u + 1) * D], probsT[:, k % 2, off + j * P:off + (j + 1) * P],
                                  v_sb[:, b * QT + j, :], j == 0, j == t)
                last.then_inc(pv_ps, 1)

            def headsT_of(pair, n):
                pe.wait_ge(head_ok, 2 * pair + 2)
                if n == 1:
                    pe.wait_ge(hT_ok, B * pair + 1)
                for u in range(QT):
                    last = nc.tensor.transpose(X_BANK[:, cols(u)], heads[:, n * QT + u, :], ident[:])
                last.then_inc(hT_ps, 1)

            def project(pair, n):
                pe.wait_ge(hT_ok, B * pair + n + 1)
                for u in range(QT):
                    last = mm(F_BANK[n][:, cols(u)], headsT[:, cols(n * QT + u)], wo_sb[:, bass.ds(pair * C, C)],
                              False, False, loose=True)
                last.then_inc(wo_ps, 1)

            pe.wait_ge(kl_ok, B)
            pe.wait_ge(v_ok, B)
            pe.wait_ge(negnull_ok, B)
            pe.wait_ge(mask_ok, 1)
            pe.wait_ge(ld["wo"], 16)
            scores(0, 0)
            scores(0, 1)

            def body(p, first, last):
                for k in range(SLOTS):
                    if k + 2 < SLOTS:
                        scores(p, k + 2)
                    elif not last:
                        scores(p + 1, k + 2 - SLOTS)
                    transposes(p, k)
                    if k > 0:
                        values(p, k - 1)
                    elif not first:
                        values(p - 1, SLOTS - 1)
                    if k in (0, 2) and not last:
                        if k == 0:
                            pe.wait_ge(wq_split, p + 2)
                        else:
                            pe.wait_ge(qlo_ok, B * p + B + 1)
                        queries(k // 2, X_BANK)
                    if k in (4, 5) and not first:
                        if k == 4 and not last:
                            pe.wait_ge(qlo_ok, B * p + 2 * B)
                        headsT_of(p - 1, k - 4)
                    if k in (6, 8) and not first:
                        project(p - 1, (k - 6) // 2)

            loop(nc.tensor, body)
            values(PAIRS - 1, SLOTS - 1)
            pe.wait_ge(place_ok, 2)
            pe.wait_ge(head_ok, 2 * PAIRS)
            for p in range(PAIRS):
                last = mm(PV_BANK[0:H, 0:C], place_v[:, p * H:(p + 1) * H], wo_sb[:, p * C:(p + 1) * C], p == 0, p == PAIRS - 1)
            last.then_inc(nout_ps, 1)
            for n in range(B):
                headsT_of(PAIRS - 1, n)
            pe.wait_ge(nullp_ok, H)
            for n in range(B):
                for u in range(QT):
                    last = nc.tensor.transpose(bank[n][0:H, cols(u)], null_prob[:, n * QT + u, :], ident[:])
                last.then_inc(npT_ps, 1)
            pe.wait_ge(nout_ok, 1)
            for n in range(B):
                project(PAIRS - 1, n)
                pe.wait_ge(npT_a if n == 0 else npT_v, 1)
                for u in range(QT):
                    last = mm(F_BANK[n][:, cols(u)], null_probT[:, cols(n * QT + u)], null_out[:], False, u == QT - 1, loose=True)
                last.then_inc(fin_ps, 1)


_INS = ["x", "cond_64", "fside_16xSxS_0", "mask_BxS_bk0", "L0_cond_wt", "L0_cond_wg", "L0_cond_w_gate", "L0_cond_w_up",
        "L0_cond_w_down", "L0_cond_sw_gate", "L0_cond_sw_up", "L0_cond_sw_down", "L1_cond_g_in",
        "L1_cond_null_attn_bias", "L1_cond_Wq", "L1_cond_Wkv", "L1_cond_Wo", "L1_cond_g_out"]


def kernel(**inputs):
    import numpy as np
    import concourse.bacc as bacc
    from concourse.bass_utils import run_bass_kernel_spmd as run

    nc = bacc.Bacc("TRN2", target_bir_lowering=False, num_devices=1)
    arrays, args = {}, []
    for name in _INS:
        a = np.ascontiguousarray(inputs[name])
        arrays[name + "_dram"] = a
        args.append(nc.dram_tensor(name + "_dram", a.shape, mybir.dt.from_np(a.dtype), kind="ExternalInput").ap())
    x = inputs["x"]
    args.append(nc.dram_tensor("out_dram", tuple(x.shape), mybir.dt.float32, kind="ExternalOutput").ap())
    moe_then_attention_program(nc, *args)
    r = run(nc, [arrays], core_ids=[0])
    return r.results[0]["out_dram"]
```

```python
import concourse.bass as bass
from concourse import mybir
from contextlib import ExitStack


def moe_then_attention_program(nc, x, cond, score_bias, keep_mask, wt, wg, w_gate, w_up, w_down,
                               sw_gate, sw_up, sw_down, g_in, null_bias, w_q, w_kv, w_o, g_out, out):
    f32, f32r, u8 = mybir.dt.float32, mybir.dt.float32r, mybir.dt.uint8
    bf16 = mybir.dt.bfloat16
    ALU, ACT, AX = mybir.AluOpType, mybir.ActivationFunctionType, mybir.AxisListType

    P = 128
    B, S, C = x.shape
    E, G = wg.shape
    M = w_gate.shape[2]
    H = null_bias.shape[0]
    D = w_kv.shape[1] // 2
    QT = S // P
    U = B * QT
    T = B * S
    PAIRS = H // 2
    EP = E // 2
    NM = EP + 1
    SHARED = EP
    WARM = 8
    NEG = -1.0e30
    EPS = 1e-5
    SLOPE = 0.01

    UNITS = [[(0, 3, 0)], [(0, 2, 0), (0, 0, 3 * P)], [(0, 1, 0), (1, 1, 2 * P)],
             [(1, 3, 0)], [(1, 2, 0), (1, 0, 3 * P)]]
    SLOTS = len(UNITS)
    before = [sum(len(v) for v in UNITS[:i]) for i in range(SLOTS + 1)]
    NU = before[SLOTS]
    TRI = P * QT * (QT + 1) // 2
    at_t = [7 * P, 8 * P, 4 * P, 0]
    at_j = [0, 4 * P, 8 * P, 7 * P]
    BLOCKS = [[(0, t, 0) for t in range(4)], [(0, t, 1) for t in (1, 2, 3)] + [(0, 3, 3)],
              [(1, t, 0) for t in range(4)], [(1, t, 1) for t in (1, 2, 3)] + [(1, 3, 3)],
              [(h, t, 2) for h in range(2) for t in (2, 3)]]
    PIECES = {3: [0], 4: [1, 3], 0: [2]}
    LAG = 4
    R = 2 * QT

    ctx = ExitStack()
    with ctx:
        def sb(name, shape, dt=f32):
            return ctx.enter_context(nc.sbuf_tensor(name, shape, dt))

        def sem(name):
            return ctx.enter_context(nc.semaphore(name))

        x_sb = sb("x_sb", [P, U, C])
        wt_sb = sb("wt_sb", [E, C])
        wg_sb = sb("wg_sb", [E, G])
        cond_sb = sb("cond_sb", [B, G])
        gate_sb = sb("gate_sb", [P, NM, P])
        up_sb = sb("up_sb", [P, NM, P])
        down_sb = sb("down_sb", [P, NM, C])
        wq_sb = sb("wq_sb", [P, PAIRS * P])
        wkv_sb = sb("wkv_sb", [P, 2 * D])
        wo_sb = sb("wo_sb", [P, PAIRS * C])
        g_in_col = sb("g_in_col", [P, 1])
        g_out_row = sb("g_out_row", [P, C])
        null_bias_row = sb("null_bias_row", [P, H])
        null_k_row = sb("null_k_row", [P, D])
        null_v_col = sb("null_v_col", [P, 1])
        keep_row = sb("keep_row", [D + 1, T], u8)
        bias_sb = sb("bias_sb", [P, 2, 2, TRI])

        ident = sb("ident", [P, P])
        earlier = sb("earlier", [P, E, E])
        pick = sb("pick", [32 + E, EP, P])
        pick_r = sb("pick_r", [32 + E, EP, P], f32r)
        row_of = sb("row_of", [2 * R, QT, P])
        row_of_r = sb("row_of_r", [2 * R, QT, P], f32r)
        minus_half = sb("minus_half", [P, QT])
        zero_bf = sb("zero_bf", [P, S], bf16)
        place_v = sb("place_v", [P, PAIRS * H])

        xT = sb("xT", [P, T])
        wtT = sb("wtT", [P, E])
        wgT = sb("wgT", [G, E])
        condT = sb("condT", [G, B, P])
        top = sb("top", [P, U])
        logit = sb("logit", [P, U, E])
        expo = sb("expo", [P, U, E])
        total = sb("total", [P, U])
        score = sb("score", [P, U, E])
        greater = sb("greater", [P, U, E * E])
        equal = sb("equal", [P, U, E * E])
        rank = sb("rank", [P, U, E])
        chosen = sb("chosen", [P, U, E])
        weight = sb("weight", [P, U, E])
        weightT = sb("weightT", [32 + E, T], f32r)
        gate = sb("gate", [P, 2, S])
        sloped = sb("sloped", [P, 2, S])
        leaky = sb("leaky", [P, 2, S])
        hidden = sb("hidden", [P, NM, T])
        x1 = sb("x1", [P, U, C])

        stats = sb("stats", [P, U, 6])
        moments = sb("moments", [P, U, 2])
        var_eps = sb("var_eps", [P, U])
        rstd = sb("rstd", [P, U])
        xn = sb("xn", [P, U, C])
        xnT_hi = sb("xnT_hi", [P, T], f32r)
        xnT_lo = sb("xnT_lo", [P, T], f32r)

        VW = D + H
        vw = sb("vw", [P, VW])
        null_prod = sb("null_prod", [P, H * D])
        wk_hi = sb("wk_hi", [P, P], f32r)
        wk_lo = sb("wk_lo", [P, P], f32r)
        vw_hi = sb("vw_hi", [P, VW], f32r)
        vw_lo = sb("vw_lo", [P, VW], f32r)
        wq_hi = sb("wq_hi", [P, 2, P], f32r)
        wq_lo = sb("wq_lo", [P, 2, P], f32r)
        k_hi = sb("k_hi", [P, T], f32r)
        k_lo = sb("k_lo", [D + 1, T], f32r)
        v_sb = sb("v_sb", [P, U, D])
        neg_null = sb("neg_null", [P, B, H, QT])
        neg_null_now = sb("neg_null_now", [P, B, R])

        q_hi = sb("q_hi", [P, T], f32r)
        q_lo = sb("q_lo", [P, T], f32r)
        q_both = [sb(f"q_both{h}", [P, T], f32r) for h in range(2)]
        q_one = [sb(f"q_one{h}", [D + 1, T], f32r) for h in range(2)]

        neg_s = sb("neg_s", [P, 2, S])
        probs = hidden[:].rearrange("p m t -> p (m t)").rearrange("p (b h c) -> p b h c", b=B, h=2)
        probsT = sb("probsT", [P, B, 2, TRI])
        neg_max = sb("neg_max", [P, B, R])
        row_sum = sb("row_sum", [P, B, R])
        null_gap = sb("null_gap", [P, B, R])
        null_exp = sb("null_exp", [P, B, R])
        full_sum = sb("full_sum", [P, B, R])
        inv_sum = sb("inv_sum", [P, B, R])
        inv_split = sb("inv_split", [P, B, 2 * R], f32r)
        inv_T = sb("inv_T", [2 * R, B, P], f32r)
        inv_wide = sb("inv_wide", [P, B, S])
        null_prob = sb("null_prob", [P, U, H])
        headsT = sb("headsT", [P, T])
        null_out = sb("null_out", [H, C])
        null_probT = sb("null_probT", [H, T])
        normed, result = xn, x_sb

        bank = [ctx.enter_context(nc.psum_tensor(f"bank{i}", [P, S], f32)) for i in range(8)]
        S_BANK, T_BANK, PV_BANK, X_BANK, F_BANK = bank[0:2], bank[2:4], bank[4], bank[5], bank[6:8]
        GATE_BANK, UP_BANK, Y_BANK, W_BANK = bank[0:2], bank[2:4], bank[4:8], bank[6:8]

        ld = {n: sem("ld_" + n) for n in ("x", "router", "gate", "up", "down", "sgate", "sup", "sdown",
                                          "wq", "wkv", "wo", "norm", "null", "null_v", "mask")}
        bias_ld = [sem("bias_ld_even"), sem("bias_ld_odd")]
        def sems(names, n=None):
            return [sem(x) if n is None else [sem(f"{x}_{i}") for i in range(n)] for x in names.split()]

        const_step, ident_ok, earlier_ok, pick_ok, row_of_ok = sems("const_step ident_ok earlier_ok pick_ok row_of_ok")
        leaky_ok, vw_step, wkv_split_ok, null_prod_ok = sems("leaky_ok vw_step wkv_split_ok null_prod_ok")
        wq_hi_ok, wq_split, rstd_ok, gap_ok, sum_ok = sems("wq_hi_ok wq_split rstd_ok gap_ok sum_ok")
        inv_hi_ok, inv_split_ok, nullp_ok = sems("inv_hi_ok inv_split_ok nullp_ok")
        bias_ok, null_now_ok = sems("bias_ok null_now_ok", 2)
        xT_ps, small_ps, logit_ps, gu_ps, wT_ps, wb_ps, y_ps = sems("xT_ps small_ps logit_ps gu_ps wT_ps wb_ps y_ps")
        xnT_ps, k_ps, v_ps, nout_ps, fin_zero = sems("xnT_ps k_ps v_ps nout_ps fin_zero")
        s_ps, t_ps, pv_ps, invT_ps, wide_ps, wo_ps, npT_ps, fin_ps = sems("s_ps t_ps pv_ps invT_ps wide_ps wo_ps npT_ps fin_ps")
        xT_a, expo_ok, sloped_ok, wTh_ok, xnTh_ok, kh_ok = sems("xT_a expo_ok sloped_ok wTh_ok xnTh_ok kh_ok")
        exp_ok, evac_a, nexp_ok, invT_ok, wide_ok, npT_ok = sems("exp_ok evac_a nexp_ok invT_ok wide_ok npT_ok")
        dve_step, warm_ok, zero_ok, xT_v, small_ok, logit_ok, weight_ok = sems("dve_step warm_ok zero_ok xT_v small_ok logit_ok weight_ok")
        t1_ok, h_ok, wTl_ok, x1_ok, var_ok, xn_ok, xnTl_ok = sems("t1_ok h_ok wTl_ok x1_ok var_ok xn_ok xnTl_ok")
        wn_ok, kl_ok, v_ok, negnull_ok, mask_ok, place_ok = sems("wn_ok kl_ok v_ok negnull_ok mask_ok place_ok")
        neg_ok, evac_v, inv_ok, head_ok, nout_ok, result_ok = sems("neg_ok evac_v inv_ok head_ok nout_ok result_ok")
        q_ps, qhi_ok, qlo_ok, q_ok = sems("q_ps qhi_ok qlo_ok q_ok", B)
        stored = sem("stored")
        dve_passed, pool_passed = sems("dve_passed pool_passed")

        tiles = lambda a: a.rearrange("b (t p) c -> p (b t) c", p=P)
        bias_view = score_bias.rearrange("h (t p) j -> p h t j", p=P)
        cols = lambda u: slice(u * P, (u + 1) * P)
        half = lambda n: slice(n * S, (n + 1) * S)

        STEPS = [(m, n) for n in range(B) for m in [SHARED] + list(range(EP))]
        WEIGHTED = [s for s, (m, n) in enumerate(STEPS) if m != SHARED]

        def stand_alone(engine, passed):
            engine.sem_inc(passed, 1)

        def known(p):
            return isinstance(p, int)

        def back(p, b, steps):
            q, c = p - (steps + 1 - b) // 2, (b + steps) % 2
            return None if known(p) and not 0 <= q < PAIRS else (q, c)

        def lagged(p, b, i, slots):
            d = (slots - i + SLOTS - 1) // SLOTS
            step = back(p, b, d)
            return None if step is None else (*step, i - slots + d * SLOTS)

        def ordinal(p, b):
            return B * p + b

        def any_step(p, b, least):
            return not known(p) or ordinal(p, b) >= least

        def evacuated(engine, p, b, i):
            g = SLOTS * b + i
            engine.wait_ge(evac_v if g % 2 else evac_a, SLOTS * p + g // 2 + 1)

        def evacuate(engine, p, b, i):
            n = ordinal(p, b)
            engine.wait_ge(t_ps, SLOTS * n + i + 1)
            if i < 2 and any_step(p, b, 2):
                engine.wait_ge(pv_ps, len(PIECES) * n - len(PIECES))
            par = (b + i) % 2
            if i == SLOTS - 1:
                to = probsT[:, b, :, at_j[2]:at_j[2] + 2 * P]
                src = T_BANK[par][:].rearrange("p (h c) -> p h c", h=2)
            else:
                to = probsT[:, b, i // 2, (i % 2) * S:(i % 2 + 1) * S]
                src = T_BANK[par][:]
            if par == 0:
                nc.scalar.activation(to, src, ACT.Copy).then_inc(evac_a, 1)
            else:
                nc.vector.tensor_copy(to, src).then_inc(evac_v, 1)

        def loop(engine, body, ahead=0):
            body(0, 0, 0)
            with engine.Fori(1, PAIRS // 2 - ahead) as turn:
                body(2 * turn - 1, 1, turn - 1)
                body(2 * turn, 0, turn)
            for p in range(PAIRS - 1 - 2 * ahead, PAIRS + 1):
                body(p, p % 2, p // 2)

        block = ctx.enter_context(nc.Block())

        @block.sync
        def _(sp):
            sp.dma_start(x_sb[:], tiles(x)).then_inc(ld["x"], 16)
            sp.dma_start(wt_sb[:], wt).then_inc(ld["router"], 16)
            sp.dma_start(wg_sb[:], wg).then_inc(ld["router"], 16)
            sp.dma_start(cond_sb[:], cond).then_inc(ld["router"], 16)
            sp.dma_start(gate_sb[:, SHARED, :], sw_gate).then_inc(ld["sgate"], 16)
            sp.dma_start(up_sb[:, SHARED, :], sw_up).then_inc(ld["sup"], 16)
            sp.dma_start(gate_sb[:, 0:EP, :].rearrange("c e (k m) -> c (e k) m", k=2),
                         w_gate.rearrange("e c m -> c e m")).then_inc(ld["gate"], 16)
            sp.dma_start(up_sb[:, 0:EP, :].rearrange("c e (k m) -> c (e k) m", k=2),
                         w_up.rearrange("e c m -> c e m")).then_inc(ld["up"], 16)
            sp.dma_start(wkv_sb[:], w_kv).then_inc(ld["wkv"], 16)
            sp.dma_start(wq_sb[:], w_q).then_inc(ld["wq"], 16)
            sp.dma_start(null_k_row[:], cond[0:1, :].broadcast_to([P, D])).then_inc(ld["null"], 16)
            sp.dma_start(null_bias_row[:], null_bias.rearrange("(a h) -> a h", a=1).broadcast_to([P, H])).then_inc(ld["null"], 16)
            sp.dma_start(down_sb[:, SHARED, :], sw_down).then_inc(ld["sdown"], 16)
            sp.dma_start(down_sb[:, 0:EP, :], w_down.rearrange("(e k) m c -> (k m) e c", k=2)).then_inc(ld["down"], 16)
            sp.dma_start(keep_row[D:D + 1, :], keep_mask.rearrange("(a b) s -> a (b s)", a=1)).then_inc(ld["mask"], 16)
            sp.dma_start(g_in_col[:], g_in.rearrange("(c a) -> c a", a=1)).then_inc(ld["norm"], 16)
            sp.dma_start(g_out_row[:], g_out.rearrange("(a c) -> a c", a=1).broadcast_to([P, C])).then_inc(ld["norm"], 16)
            for k in range(2):
                sp.dma_start(null_v_col[k * D:(k + 1) * D, :], cond[1:2, :].rearrange("a d -> d a")).then_inc(ld["null_v"], 16)

            def load_bias(p, par):
                for t in range(QT):
                    w = (t + 1) * P
                    sp.dma_start(bias_sb[:, par, :, at_t[t]:at_t[t] + w],
                                 bias_view[:, bass.ds(2 * p, 2), t, 0:w]).then_inc(bias_ld[par], 16)

            def copy_queries(p, b):
                sp.wait_ge(qhi_ok[b], p + 1)
                sp.wait_ge(qlo_ok[b], p + 1)
                if not known(p) or p > 0:
                    sp.wait_ge(s_ps, SLOTS * ordinal(p - 1, b) + SLOTS)
                for h in range(2):
                    own = slice(h * D, (h + 1) * D)
                    for to, rows, part in ((q_both[h], slice(0, D), q_hi), (q_both[h], slice(D, P), q_lo),
                                           (q_one[h], slice(0, D), q_hi)):
                        sp.dma_start(to[rows, half(b)].bitcast(f32), part[own, half(b)].bitcast(f32)).then_inc(q_ok[b], 16)

            load_bias(0, 0)
            sp.dma_start(wo_sb[:].rearrange("p (a c) -> p a c", c=C), w_o.rearrange("(a p) c -> p a c", p=P)).then_inc(ld["wo"], 16)
            load_bias(1, 1)
            copy_queries(0, 0)
            copy_queries(0, 1)

            def body(p, par, j):
                if known(p) and p + 1 >= PAIRS:
                    return
                for b in range(B):
                    copy_queries(p + 1, b)
                if not known(p) or p + 2 < PAIRS:
                    sp.wait_ge(neg_ok, NU * ordinal(p, B - 1) + NU)
                    load_bias(p + 2, par)

            loop(nc.sync, body, ahead=1)
            for n in range(B):
                sp.wait_ge(result_ok, n + 1)
                sp.dma_start(tiles(out)[:, n * QT:(n + 1) * QT, :], result[:, n * QT:(n + 1) * QT, :]).then_inc(stored, 16)
            sp.wait_ge(stored, 16 * B)

        @block.gpsimd
        def _(pool):
            steps = [0]

            def step(ins):
                steps[0] += 1
                ins.then_inc(const_step, 1)
                pool.wait_ge(const_step, steps[0])

            step(pool.memset(ident[:], 0.0))
            pool.affine_select(out=ident[:], in_=ident[:], compare_op=ALU.not_equal, fill=1.0, base=0,
                               pattern=[[-1, P]], channel_multiplier=1).then_inc(ident_ok, 1)
            step(pool.memset(earlier[:], 1.0))
            pool.affine_select(out=earlier[:], in_=earlier[:], compare_op=ALU.is_gt, fill=0.0, base=0,
                               pattern=[[1, E], [-1, E]], channel_multiplier=0).then_inc(earlier_ok, 1)
            step(pool.memset(pick[:], 0.0))
            for base in (0, -32):
                step(pool.affine_select(out=pick[:], in_=pick[:], compare_op=ALU.not_equal, fill=1.0, base=base,
                                        pattern=[[-2, EP], [-1, 2], [0, M]], channel_multiplier=1))
            pool.tensor_copy(pick_r[:], pick[:]).then_inc(pick_ok, 1)

            def leaky_step(s):
                pool.wait_ge(sloped_ok, s + 1)
                if s >= 2:
                    pool.wait_ge(t1_ok, s - 1)
                pool.tensor_tensor(leaky[:, s % 2, :], gate[:, s % 2, :], sloped[:, s % 2, :], ALU.subtract).then_inc(leaky_ok, 1)

            def split_wq(p, par):
                own = wq_sb[:, bass.ds(p * P, P)]
                pool.tensor_copy(wq_hi[:, par, :], own).then_inc(wq_hi_ok, 1)
                pool.wait_ge(wq_hi_ok, p + 1)
                stand_alone(pool, pool_passed)
                pool.tensor_tensor(wq_lo[:, par, :], own, wq_hi[:, par, :].bitcast(f32), ALU.subtract).then_inc(wq_split, 1)

            def causal(par, j):
                pool.wait_ge(bias_ld[par], 16 * QT * j + 16 * QT)
                stand_alone(pool, pool_passed)
                for t in range(QT):
                    at = at_t[t] + t * P
                    diagonal = bias_sb[:, par, :, at:at + P]
                    pool.affine_select(out=diagonal, in_=diagonal, compare_op=ALU.is_ge, fill=NEG, base=0,
                                       pattern=[[0, 2], [-1, P]], channel_multiplier=1).then_inc(bias_ok[par], 1)

            def rstd_of(count, own):
                pool.wait_ge(var_ok, count)
                pool.tensor_tensor(rstd[:, own], var_eps[:, own], minus_half[:, 0:own.stop - own.start], ALU.pow).then_inc(rstd_ok, 1)

            pool.wait_ge(ld["wkv"], 16)
            for k in range(2):
                pool.tensor_copy(wk_hi[:, k * D:(k + 1) * D], wkv_sb[:, 0:D]).then_inc(vw_step, 1)
            pool.tensor_copy(vw[:, 0:D], wkv_sb[:, D:2 * D]).then_inc(vw_step, 1)
            pool.wait_ge(vw_step, 2)
            for k in range(2):
                pool.tensor_tensor(wk_lo[:, k * D:(k + 1) * D], wkv_sb[:, 0:D],
                                   wk_hi[:, k * D:(k + 1) * D].bitcast(f32), ALU.subtract).then_inc(wkv_split_ok, 1)
            pool.wait_ge(ld["wq"], 16)
            pool.wait_ge(ld["null"], 32)
            pool.tensor_tensor(null_prod[:].rearrange("p (h d) -> p h d", d=D), wq_sb[:].rearrange("p (h d) -> p h d", d=D),
                               null_k_row[:].unsqueeze(1).broadcast_to([P, H, D]), ALU.mult).then_inc(null_prod_ok, 1)
            for s in range(4):
                leaky_step(s)
            split_wq(0, 0)
            leaky_step(4)
            leaky_step(5)
            pool.wait_ge(wn_ok, 1)
            pool.wait_ge(vw_step, 3)
            pool.tensor_copy(vw_hi[:], vw[:]).then_inc(vw_step, 1)
            leaky_step(6)
            pool.wait_ge(vw_step, 4)
            pool.tensor_tensor(vw_lo[:], vw[:], vw_hi[:].bitcast(f32), ALU.subtract).then_inc(wkv_split_ok, 1)
            for s in range(7, len(STEPS)):
                leaky_step(s)
            split_wq(1, 1)
            for q in range(2):
                rstd_of(q + 1, slice(q * QT // 2, (q + 1) * QT // 2))
            step(pool.memset(row_of[:], 0.0))
            for base in (0, -R):
                step(pool.affine_select(out=row_of[:], in_=row_of[:], compare_op=ALU.not_equal, fill=1.0, base=base,
                                        pattern=[[-1, QT], [-QT, 2], [0, D]], channel_multiplier=1))
            for q in range(2, 2 * B):
                rstd_of(q + 1, slice(q * QT // 2, (q + 1) * QT // 2))
            causal(0, 0)
            for n in range(B):
                pool.wait_ge(negnull_ok, n + 1)
                pool.tensor_copy(neg_null_now[:, n, :].rearrange("p (h t) -> p h t", h=2), neg_null[:, n, 0:2, :]).then_inc(null_now_ok[n], 1)
            pool.tensor_copy(row_of_r[:], row_of[:]).then_inc(row_of_ok, 1)

            def inverses(p, b):
                n = ordinal(p, b)
                pool.wait_ge(neg_ok, NU * n + NU)
                pool.tensor_tensor(null_gap[:, b, :], neg_max[:, b, :], neg_null_now[:, b, :], ALU.subtract).then_inc(gap_ok, 1)
                if not known(p) or p + 1 < PAIRS:
                    pool.wait_ge(gap_ok, n + 1)
                    stand_alone(pool, pool_passed)
                    pool.tensor_copy(neg_null_now[:, b, :].rearrange("p (h t) -> p h t", h=2),
                                     neg_null[:, b, bass.ds(2 * p + 2, 2), :]).then_inc(null_now_ok[b], 1)
                pool.wait_ge(nexp_ok, n + 1)
                pool.tensor_tensor(full_sum[:, b, :], row_sum[:, b, :], null_exp[:, b, :], ALU.add).then_inc(sum_ok, 1)
                pool.wait_ge(inv_ok, n + 1)
                stand_alone(pool, pool_passed)
                pool.tensor_copy(inv_split[:, b, 0:R], inv_sum[:, b, :]).then_inc(inv_hi_ok, 1)
                pool.wait_ge(inv_hi_ok, n + 1)
                pool.tensor_tensor(inv_split[:, b, R:2 * R], inv_sum[:, b, :], inv_split[:, b, 0:R].bitcast(f32),
                                   ALU.subtract).then_inc(inv_split_ok, 1)
                pool.tensor_tensor(null_prob[:, b * QT:(b + 1) * QT, bass.ds(2 * p, 2)].rearrange("p t h -> p h t"),
                                   null_exp[:, b, :].rearrange("p (h t) -> p h t", h=2),
                                   inv_sum[:, b, :].rearrange("p (h t) -> p h t", h=2), ALU.mult).then_inc(nullp_ok, 1)

            def body(p, par, j):
                if known(p) and p == PAIRS:
                    return
                if not known(p) or p + 1 < PAIRS:
                    causal(1 - par, j + par)
                if not known(p) or p + 2 < PAIRS:
                    pool.wait_ge(q_ps[B - 1], p + 1)
                    stand_alone(pool, pool_passed)
                    split_wq(p + 2, par)
                for b in range(B):
                    inverses(p, b)

            loop(nc.gpsimd, body, ahead=1)
            for n in range(B):
                rstd_of(2 * B + n + 1, slice(n * QT, (n + 1) * QT))

        @block.scalar
        def _(act):
            act.wait_ge(xT_ps, 1)
            nc.scalar.activation(xT[:, half(0)], bank[0][:], ACT.Copy).then_inc(xT_a, 1)

            def gate_step(s):
                act.wait_ge(gu_ps, s + 1)
                if s >= 2:
                    act.wait_ge(leaky_ok, s - 1)
                nc.scalar.activation(gate[:, s % 2, :], GATE_BANK[s % 2][:], ACT.Relu)
                nc.scalar.activation(sloped[:, s % 2, :], GATE_BANK[s % 2][:], ACT.Relu, scale=-SLOPE).then_inc(sloped_ok, 1)

            act.wait_ge(logit_ok, 1)
            nc.scalar.activation(expo[:], logit[:], ACT.Exp, scale=0.5).then_inc(expo_ok, 1)
            for s in range(len(STEPS)):
                if s == 4:
                    for n in range(B):
                        act.wait_ge(wT_ps, n + 1)
                        nc.scalar.activation(weightT[0:E, half(n)], W_BANK[n][0:E, :], ACT.Copy).then_inc(wTh_ok, 1)
                gate_step(s)

            def tokens_hi(n, psum):
                act.wait_ge(xnT_ps, n + 1)
                nc.scalar.activation(xnT_hi[:, half(n)], psum[:], ACT.Copy, scale=g_in_col[:, 0:1]).then_inc(xnTh_ok, 1)

            def keys_hi(n, psum):
                act.wait_ge(k_ps, n + 1)
                nc.scalar.activation(k_hi[:, half(n)], psum[:], ACT.Copy).then_inc(kh_ok, 1)

            def queries_hi(p, b, psum):
                act.wait_ge(q_ps[b], p + 1)
                if not known(p) or p > 0:
                    act.wait_ge(q_ok[b], 96 * p)
                nc.scalar.activation(q_hi[:, half(b)], psum[:], ACT.Copy, scale=float(D) ** -0.5).then_inc(qhi_ok[b], 1)

            act.wait_ge(ld["norm"], 32)
            tokens_hi(0, bank[0])
            keys_hi(0, bank[2])
            queries_hi(0, 0, bank[4])
            tokens_hi(1, bank[1])
            keys_hi(1, bank[3])
            queries_hi(0, 1, bank[5])

            def exp_slot(p, b, i):
                n = ordinal(p, b)
                for at, (h, t, off) in enumerate(UNITS[i]):
                    w = (t + 1) * P
                    act.wait_ge(neg_ok, NU * n + before[i] + at + 1)
                    if i == 0 and any_step(p, b, 2):
                        act.wait_ge(t_ps, SLOTS * n - SLOTS)
                    nc.scalar.activation(probs[:, b, h, at_t[t]:at_t[t] + w], neg_s[:, (b + i) % 2, off:off + w], ACT.Exp,
                                         bias=neg_max[:, b, h * QT + t:h * QT + t + 1], scale=-1.0,
                                         accum_out=row_sum[:, b, h * QT + t:h * QT + t + 1]).then_inc(exp_ok, 1)

            def body(p, par, j):
                for b in range(B):
                    for i in range(SLOTS):
                        last, two = back(p, b, 1), back(p, b, 2)
                        if last and i == 4:
                            act.wait_ge(invT_ps, ordinal(*last) + 1)
                            nc.scalar.activation(inv_T[:, last[1], :], X_BANK[0:2 * R, 0:P], ACT.Copy).then_inc(invT_ok, 1)
                        if two and i == 0:
                            act.wait_ge(wide_ps, ordinal(*two) + 1)
                            nc.scalar.activation(inv_wide[:, two[1], :], X_BANK[:], ACT.Copy).then_inc(wide_ok, 1)
                        done = lagged(p, b, i, LAG)
                        if done and (done[1] + done[2]) % 2 == 0:
                            evacuate(act, *done)
                        if not known(p) or p < PAIRS:
                            exp_slot(p, b, i)
                        if i == 2 and (not known(p) or p + 1 < PAIRS):
                            queries_hi(p + 1, b, X_BANK)
                        if last and i == 0:
                            act.wait_ge(gap_ok, ordinal(*last) + 1)
                            nc.scalar.activation(null_exp[:, last[1], :], null_gap[:, last[1], :], ACT.Exp).then_inc(nexp_ok, 1)
                        if known(p) and p == PAIRS and i == 0:
                            act.wait_ge(npT_ps, b + 1)
                            nc.scalar.activation(null_probT[:, half(b)], S_BANK[b][0:H, :], ACT.Copy).then_inc(npT_ok, 1)

            loop(nc.scalar, body)

        @block.vector
        def _(dve):
            steps = [0]

            def step(ins):
                steps[0] += 1
                ins.then_inc(dve_step, 1)
                dve.wait_ge(dve_step, steps[0])

            nc.vector.memset(zero_bf[:].bitcast(f32), 0.0).then_inc(warm_ok, 1)
            nc.vector.memset(minus_half[:], -0.5)
            nc.vector.memset(place_v[:], 0.0)
            for h in range(2):
                nc.vector.memset(q_one[h][D:D + 1, :].bitcast(f32), 1.0).then_inc(zero_ok, 1)
            step(nc.vector.memset(weightT[:].bitcast(f32), 0.0))
            dve.wait_ge(xT_ps, 2)
            nc.vector.tensor_copy(xT[:, half(1)], bank[1][:]).then_inc(xT_v, 1)
            dve.wait_ge(small_ps, 1)
            nc.vector.tensor_copy(wtT[:], bank[2][:, 0:E])
            nc.vector.tensor_copy(wgT[:], bank[2][0:G, E:2 * E])
            nc.vector.tensor_copy(condT[:], bank[2][0:G, 2 * E:2 * E + B].unsqueeze(2).broadcast_to([G, B, P])).then_inc(small_ok, 1)

            dve.wait_ge(logit_ps, 1)
            wide = lambda a: a.unsqueeze(2).broadcast_to([*a.shape, E])
            logits = [Y_BANK[n][:, 0:QT * E].rearrange("p (u e) -> p u e", e=E) for n in range(B)]
            own = [slice(n * QT, (n + 1) * QT) for n in range(B)]
            for n in range(B):
                last = nc.vector.reduce_max(top[:, own[n]], logits[n], AX.X)
            step(last)
            for n in range(B):
                last = nc.vector.tensor_tensor(logit[:, own[n], :], logits[n], wide(top[:, own[n]]), ALU.subtract)
            last.then_inc(logit_ok, 1)

            def t1_step(s):
                m, n = STEPS[s]
                dve.wait_ge(leaky_ok, s + 1)
                ins = nc.vector.tensor_tensor(hidden[:, m, half(n)], leaky[:, s % 2, :], UP_BANK[s % 2][:], ALU.mult)
                ins.then_inc(t1_ok, 1)

            dve.wait_ge(expo_ok, 1)
            step(nc.vector.reduce_sum(total[:], expo[:], AX.X))
            step(nc.vector.reciprocal(total[:], total[:]))
            step(nc.vector.tensor_tensor(score[:], expo[:], wide(total[:]), ALU.mult))
            other = lambda a: a.unsqueeze(2).broadcast_to([P, U, E, E])
            own = lambda a: a.unsqueeze(3).broadcast_to([P, U, E, E])
            four = lambda a: a.rearrange("p u (e f) -> p u e f", f=E)
            nc.vector.tensor_tensor(four(greater[:]), other(score[:]), own(score[:]), ALU.is_gt)
            step(nc.vector.tensor_tensor(four(equal[:]), other(score[:]), own(score[:]), ALU.is_equal))
            dve.wait_ge(earlier_ok, 1)
            step(nc.vector.tensor_tensor(equal[:], equal[:], earlier[:].rearrange("p e f -> p (e f)").unsqueeze(1)
                                         .broadcast_to([P, U, E * E]), ALU.mult))
            t1_step(0)
            step(nc.vector.tensor_tensor(equal[:], equal[:], greater[:], ALU.add))
            step(nc.vector.reduce_sum(rank[:], four(equal[:]), AX.X))
            step(nc.vector.scalar_tensor_tensor(out=chosen[:], in0=rank[:], scalar=1.5, in1=score[:],
                                                op0=ALU.is_lt, op1=ALU.mult))
            t1_step(1)
            step(nc.vector.reduce_sum(total[:], chosen[:], AX.X))
            step(nc.vector.tensor_scalar_add(total[:], total[:], 1e-20))
            step(nc.vector.reciprocal(total[:], total[:]))
            nc.vector.tensor_tensor(weight[:], chosen[:], wide(total[:]), ALU.mult).then_inc(weight_ok, 1)
            t1_step(2)
            t1_step(3)
            for n in range(B):
                dve.wait_ge(wTh_ok, n + 1)
                nc.vector.tensor_tensor(weightT[32:32 + E, half(n)], W_BANK[n][0:E, :],
                                        weightT[0:E, half(n)].bitcast(f32), ALU.subtract).then_inc(wTl_ok, 1)

            def h_step(r):
                m, n = STEPS[WEIGHTED[r]]
                dve.wait_ge(wb_ps, r + 1)
                dve.wait_ge(t1_ok, WEIGHTED[r] + 1)
                nc.vector.tensor_tensor(hidden[:, m, half(n)], hidden[:, m, half(n)], W_BANK[r % 2][:], ALU.mult).then_inc(h_ok, 1)

            def norm_tokens(q):
                own = slice(q * QT // 2, (q + 1) * QT // 2)
                tiles_q = range(q * QT // 2, (q + 1) * QT // 2)
                dve.wait_ge(y_ps, q + 1)
                made = Y_BANK[q][:, 0:QT // 2 * C].rearrange("p (u c) -> p u c", c=C)
                nc.vector.tensor_tensor(x1[:, own, :], x_sb[:, own, :], made, ALU.add).then_inc(x1_ok, 1)
                dve.wait_ge(x1_ok, q + 1)
                for u in tiles_q:
                    last = nc.vector.bn_stats(stats[:, u, :], x1[:, u, :])
                step(last)
                for u in tiles_q:
                    last = nc.vector.bn_aggr(moments[:, u, :], stats[:, u, :])
                step(last)
                nc.vector.tensor_scalar_add(var_eps[:, own], moments[:, own, 1], EPS).then_inc(var_ok, 1)

            def scale_tokens(q):
                dve.wait_ge(rstd_ok, q + 1)
                for u in range(q * QT // 2, (q + 1) * QT // 2):
                    last = nc.vector.tensor_scalar(xn[:, u, :], x1[:, u, :], moments[:, u, 0:1], rstd[:, u:u + 1],
                                                   ALU.subtract, ALU.mult)
                last.then_inc(xn_ok, 1)

            def queries_lo(p, b, psum):
                dve.wait_ge(qhi_ok[b], p + 1)
                if not known(p) or p > 0:
                    dve.wait_ge(q_ok[b], 96 * p)
                nc.vector.scalar_tensor_tensor(out=q_lo[:, half(b)], in0=psum[:], scalar=float(D) ** -0.5,
                                               in1=q_hi[:, half(b)].bitcast(f32), op0=ALU.mult,
                                               op1=ALU.subtract).then_inc(qlo_ok[b], 1)

            def tokens_lo(n, psum):
                dve.wait_ge(xnTh_ok, n + 1)
                nc.vector.scalar_tensor_tensor(out=xnT_lo[:, half(n)], in0=psum[:], scalar=g_in_col[:, 0:1],
                                               in1=xnT_hi[:, half(n)].bitcast(f32), op0=ALU.mult,
                                               op1=ALU.subtract).then_inc(xnTl_ok, 1)

            def keys_lo(n, psum, made):
                dve.wait_ge(kh_ok, n + 1)
                nc.vector.tensor_tensor(k_lo[0:D, half(n)], psum[0:D, :], k_hi[0:D, half(n)].bitcast(f32),
                                        ALU.subtract).then_inc(kl_ok, 1)
                dve.wait_ge(v_ps, n + 1)
                made = made[:, 0:QT * VW].rearrange("p (u w) -> p u w", w=VW)
                nc.vector.tensor_copy(v_sb[:, n * QT:(n + 1) * QT, :], made[:, :, 0:D]).then_inc(v_ok, 1)
                nc.vector.scalar_tensor_tensor(
                    out=neg_null[:, n].rearrange("p h t -> p t h"), in0=made[:, :, D:VW],
                    scalar=-float(D) ** -0.5, in1=null_bias_row[:].unsqueeze(1).broadcast_to([P, QT, H]),
                    op0=ALU.mult, op1=ALU.subtract).then_inc(negnull_ok, 1)

            dve.wait_ge(null_prod_ok, 1)
            nc.vector.reduce_sum(vw[:, D:VW], null_prod[:].rearrange("p (h d) -> p h d", d=D), AX.X).then_inc(wn_ok, 1)
            dve.wait_ge(ld["mask"], 16)
            nc.vector.tensor_scalar(k_lo[D:D + 1, :], keep_row[D:D + 1, :], -NEG, NEG, ALU.mult, ALU.add).then_inc(mask_ok, 1)
            dve.wait_ge(ld["null_v"], 32)
            for k in range(2):
                nc.vector.tensor_copy(place_v[k * D:(k + 1) * D, k::H + 2],
                                      null_v_col[k * D:(k + 1) * D, 0:1].broadcast_to([D, PAIRS])).then_inc(place_ok, 1)
            for r in range(len(WEIGHTED)):
                if r + 4 < len(STEPS):
                    t1_step(r + 4)
                h_step(r)
            for q in range(2 * B):
                norm_tokens(q)
                if q % 2:
                    scale_tokens(q - 1)
                    scale_tokens(q)
                if q == 1:
                    tokens_lo(0, bank[0])
            keys_lo(0, bank[2], bank[6])
            queries_lo(0, 0, bank[4])
            tokens_lo(1, bank[1])
            keys_lo(1, bank[3], bank[7])
            queries_lo(0, 1, bank[5])

            def score_slot(p, b, i, par, j):
                n = ordinal(p, b)
                dve.wait_ge(s_ps, SLOTS * n + i + 1)
                if any_step(p, b, 1) or i >= 2:
                    dve.wait_ge(exp_ok, NU * n + before[i] - len(UNITS[i - 1]))
                if i == 0:
                    if b == 0:
                        dve.wait_ge(bias_ok[par], QT * j + QT)
                    dve.wait_ge(null_now_ok[b], p + 1)
                stand_alone(dve, dve_passed)
                for h, t, off in UNITS[i]:
                    w = (t + 1) * P
                    r = h * QT + t
                    nc.vector.tensor_tensor_reduce(
                        out=neg_s[:, (b + i) % 2, off:off + w], in0=S_BANK[(b + i) % 2][:, off:off + w],
                        in1=bias_sb[:, par, h, at_t[t]:at_t[t] + w], scale=-1.0, scalar=neg_null_now[:, b, r:r + 1],
                        op0=ALU.add, op1=ALU.min, accum_out=neg_max[:, b, r:r + 1]).then_inc(neg_ok, 1)

            def invert(p, b):
                dve.wait_ge(sum_ok, ordinal(p, b) + 1)
                nc.vector.reciprocal(inv_sum[:, b, :], full_sum[:, b, :]).then_inc(inv_ok, 1)

            def normalise(p, b):
                dve.wait_ge(pv_ps, len(PIECES) * ordinal(p, b) + len(PIECES))
                dve.wait_ge(wide_ok, ordinal(p, b) + 1)
                nc.vector.tensor_tensor(headsT[:, half(b)], PV_BANK[:], inv_wide[:, b, :], ALU.mult).then_inc(head_ok, 1)

            def last_norm(n):
                own = slice(n * QT, (n + 1) * QT)
                dve.wait_ge(fin_ps, n + 1)
                for u in range(QT):
                    last = nc.vector.bn_stats(stats[:, n * QT + u, :], F_BANK[n][:, cols(u)])
                step(last)
                for u in range(n * QT, (n + 1) * QT):
                    last = nc.vector.bn_aggr(moments[:, u, :], stats[:, u, :])
                step(last)
                nc.vector.tensor_scalar_add(var_eps[:, own], moments[:, own, 1], EPS).then_inc(var_ok, 1)

            def last_scale(n):
                own = slice(n * QT, (n + 1) * QT)
                dve.wait_ge(rstd_ok, 2 * B + n + 1)
                for u in range(n * QT, (n + 1) * QT):
                    last = nc.vector.tensor_scalar(normed[:, u, :], F_BANK[n][:, cols(u % QT)], moments[:, u, 0:1],
                                                   rstd[:, u:u + 1], ALU.subtract, ALU.mult)
                step(last)
                step(nc.vector.tensor_tensor(result[:, own, :], normed[:, own, :],
                                             g_out_row[:].unsqueeze(1).broadcast_to([P, QT, C]), ALU.mult))
                nc.vector.tensor_tensor(result[:, own, :], result[:, own, :], x1[:, own, :], ALU.add).then_inc(result_ok, 1)

            def body(p, par, j):
                for b in range(B):
                    for i in range(SLOTS):
                        one, two = back(p, b, 1), back(p, b, 2)
                        if two and i == 0:
                            normalise(*two)
                        if not known(p) or p < PAIRS:
                            score_slot(p, b, i, par, j)
                        done = lagged(p, b, i, LAG)
                        if done and (done[1] + done[2]) % 2 == 1:
                            evacuate(dve, *done)
                        if one and i == 1:
                            invert(*one)
                        if i == 2 and (not known(p) or p + 1 < PAIRS):
                            queries_lo(p + 1, b, X_BANK)
                        if known(p) and p == 0 and b == 1 and i == 2:
                            dve.wait_ge(nout_ps, 1)
                            nc.vector.tensor_copy(null_out[:], bank[6][0:H, 0:C]).then_inc(nout_ok, 1)
                    if known(p) and p == PAIRS and b == 1:
                        last_norm(0)
                        last_scale(0)
                        last_norm(1)
                        last_scale(1)

            loop(nc.vector, body)

        @block.tensor
        def _(pe):
            def mm(o, a, b, start=True, stop=True, loose=False):
                return nc.tensor.matmul(o, a, b, start=start, stop=stop, skip_group_check=loose)

            def three(o, a_hi, a_lo, b_hi, b_lo):
                mm(o, a_hi, b_hi, True, False)
                mm(o, a_lo, b_hi, False, False)
                return mm(o, a_hi, b_lo, False, True)

            pe.wait_ge(warm_ok, 1)
            for _ in range(WARM):
                mm(bank[7][:], zero_bf[:, 0:P], zero_bf[:])
            pe.wait_ge(ident_ok, 1)
            pe.wait_ge(ld["x"], 16)
            for n in range(B):
                for u in range(QT):
                    last = nc.tensor.transpose(bank[n][:, cols(u)], x_sb[:, n * QT + u, :], ident[:])
                last.then_inc(xT_ps, 1)
            pe.wait_ge(ld["router"], 48)
            nc.tensor.transpose(bank[2][:, 0:E], wt_sb[:], ident[0:E, 0:E])
            nc.tensor.transpose(bank[2][0:G, E:2 * E], wg_sb[:], ident[0:E, 0:E])
            nc.tensor.transpose(bank[2][0:G, 2 * E:2 * E + B], cond_sb[:], ident[0:B, 0:B]).then_inc(small_ps, 1)
            pe.wait_ge(small_ok, 1)
            pe.wait_ge(xT_a, 1)
            pe.wait_ge(xT_v, 1)
            for n in range(B):
                mm(Y_BANK[n][:, 0:QT * E].rearrange("p (u e) -> p u e", e=E), condT[:, n, :],
                   wgT[:].unsqueeze(1).broadcast_to([G, QT, E]), True, False, loose=True)
                for u in range(QT):
                    last = mm(Y_BANK[n][:, u * E:(u + 1) * E], xT[:, cols(n * QT + u)], wtT[:], False, u == QT - 1, loose=True)
            last.then_inc(logit_ps, 1)

            def gate_up(s):
                m, n = STEPS[s]
                if s == 0:
                    pe.wait_ge(ld["sgate"], 16)
                    pe.wait_ge(ld["sup"], 16)
                if s == 1:
                    pe.wait_ge(ld["gate"], 16)
                    pe.wait_ge(ld["up"], 16)
                if s >= 2:
                    pe.wait_ge(sloped_ok, s - 1)
                mm(GATE_BANK[s % 2][:], gate_sb[:, m, :], xT[:, half(n)])
                if s >= 2:
                    pe.wait_ge(t1_ok, s - 1)
                mm(UP_BANK[s % 2][:], up_sb[:, m, :], xT[:, half(n)]).then_inc(gu_ps, 1)

            def weights_wide(r):
                m, n = STEPS[WEIGHTED[r]]
                pe.wait_ge(wTl_ok, B)
                if r >= 2:
                    pe.wait_ge(h_ok, r - 1)
                mm(W_BANK[r % 2][:], pick_r[:, m, :], weightT[:, half(n)]).then_inc(wb_ps, 1)

            def down(n, part):
                pe.wait_ge(h_ok, EP * (n + 1))
                if n == 0 and part == 0:
                    pe.wait_ge(ld["down"], 16)
                    pe.wait_ge(ld["sdown"], 16)
                q = 2 * n + part
                for u in range(QT // 2):
                    for m in range(NM):
                        last = mm(Y_BANK[q][:, cols(u)], hidden[:, m, cols(q * QT // 2 + u)], down_sb[:, m, :], m == 0, m == NM - 1)
                last.then_inc(y_ps, 1)

            def tokensT(n, psum):
                pe.wait_ge(xn_ok, 2 * n + 2)
                for u in range(QT):
                    last = nc.tensor.transpose(psum[:, cols(u)], xn[:, n * QT + u, :], ident[:])
                last.then_inc(xnT_ps, 1)

            def queries(p, b, par, psum):
                three(psum[:], wq_hi[:, par, :], wq_lo[:, par, :], xnT_hi[:, half(b)], xnT_lo[:, half(b)]).then_inc(q_ps[b], 1)

            def keys(n, psum):
                three(psum[:], wk_hi[:], wk_lo[:], xnT_hi[:, half(n)], xnT_lo[:, half(n)]).then_inc(k_ps, 1)

            def values_made(n, psum):
                for u in range(QT):
                    own = cols(n * QT + u)
                    last = three(psum[:, u * VW:(u + 1) * VW], xnT_hi[:, own], xnT_lo[:, own], vw_hi[:], vw_lo[:])
                last.then_inc(v_ps, 1)

            for s in range(4):
                gate_up(s)
            pe.wait_ge(weight_ok, 1)
            for n in range(B):
                for u in range(QT):
                    last = nc.tensor.transpose(W_BANK[n][0:E, cols(u)], weight[:, n * QT + u, :], ident[:])
                last.then_inc(wT_ps, 1)
            pe.wait_ge(pick_ok, 1)
            for s in range(4, len(STEPS)):
                gate_up(s)
                weights_wide(s - 4)
            weights_wide(6)
            down(0, 0)
            weights_wide(7)
            down(0, 1)
            down(1, 0)
            pe.wait_ge(sloped_ok, len(STEPS))
            tokensT(0, bank[0])
            down(1, 1)
            pe.wait_ge(t1_ok, len(STEPS))
            pe.wait_ge(h_ok, len(WEIGHTED))
            pe.wait_ge(wkv_split_ok, 3)
            pe.wait_ge(wq_split, 1)
            pe.wait_ge(xnTl_ok, 1)
            keys(0, bank[2])
            pe.wait_ge(x1_ok, 3)
            values_made(0, bank[6])
            queries(0, 0, 0, bank[4])
            tokensT(1, bank[1])
            pe.wait_ge(xnTl_ok, 2)
            keys(1, bank[3])
            values_made(1, bank[7])
            queries(0, 1, 0, bank[5])

            def scores(p, b, i):
                n = ordinal(p, b)
                if i == 0:
                    pe.wait_ge(q_ok[b], 96 * p + 96)
                if any_step(p, b, 1) or i >= 2:
                    pe.wait_ge(neg_ok, NU * n + before[i] - len(UNITS[i - 1]))
                for h, t, off in UNITS[i]:
                    w = (t + 1) * P
                    o = S_BANK[(b + i) % 2][:, off:off + w]
                    mm(o, q_both[h][:, cols(b * QT + t)], k_hi[:, b * S:b * S + w], True, False)
                    last = mm(o, q_one[h][:, cols(b * QT + t)], k_lo[:, b * S:b * S + w], False, True)
                last.then_inc(s_ps, 1)

            def transposes(p, b, i):
                n = ordinal(p, b)
                pe.wait_ge(exp_ok, NU * n + before[3 if i < 2 else SLOTS])
                if any_step(p, b, 1) or i >= 2:
                    evacuated(pe, *lagged_any(p, b, i, 2))
                for c, (h, t, k) in enumerate(BLOCKS[i]):
                    at = at_t[t] + k * P
                    last = nc.tensor.transpose(T_BANK[(b + i) % 2][:, cols(c)], probs[:, b, h, at:at + P], ident[:])
                last.then_inc(t_ps, 1)

            def lagged_any(p, b, i, slots):
                d = (slots - i + SLOTS - 1) // SLOTS
                return p - (d + 1 - b) // 2, (b + d) % 2, i - slots + d * SLOTS

            def weigh_values(p, b, piece):
                n = ordinal(p, b)
                tiles_k = PIECES[piece]
                if tiles_k == [0]:
                    for i in (0, 2):
                        evacuated(pe, p, b, i)
                    if any_step(p, b, 1):
                        pe.wait_ge(head_ok, n)
                else:
                    for i in ((1, 3) if piece == 4 else (4,)):
                        evacuated(pe, p, b, i)
                for k in tiles_k:
                    w = (QT - k) * P
                    for h in range(2):
                        last = mm(PV_BANK[h * D:(h + 1) * D, k * P:S], v_sb[:, b * QT + k, :],
                                  probsT[:, b, h, at_j[k]:at_j[k] + w], k == 0, k == 2, loose=True)
                last.then_inc(pv_ps, 1)

            def inverseT(p, b):
                pe.wait_ge(inv_split_ok, ordinal(p, b) + 1)
                nc.tensor.transpose(X_BANK[0:2 * R, 0:P], inv_split[:, b, :].bitcast(f32), ident[:]).then_inc(invT_ps, 1)

            def inverse_wide(p, b):
                pe.wait_ge(invT_ok, ordinal(p, b) + 1)
                for t in range(QT):
                    last = mm(X_BANK[:, cols(t)], row_of_r[:, t, :], inv_T[:, b, :])
                last.then_inc(wide_ps, 1)

            def project(p, b):
                pe.wait_ge(head_ok, ordinal(p, b) + 1)
                for u in range(QT):
                    last = mm(F_BANK[b][:, cols(u)], headsT[:, cols(b * QT + u)], wo_sb[:, bass.ds(p * C, C)],
                              False, False, loose=True)
                last.then_inc(wo_ps, 1)

            pe.wait_ge(kl_ok, B)
            pe.wait_ge(v_ok, B)
            pe.wait_ge(negnull_ok, B)
            pe.wait_ge(qlo_ok[0], 1)
            pe.wait_ge(mask_ok, 1)
            pe.wait_ge(zero_ok, 2)
            pe.wait_ge(row_of_ok, 1)

            def body(p, par, j):
                for b in range(B):
                    for i in range(SLOTS):
                        one, two = back(p, b, 1), back(p, b, 2)
                        if not known(p) or p < PAIRS:
                            scores(p, b, i)
                        done = lagged(p, b, i, LAG)
                        if done:
                            transposes(*done)
                        if done and done[2] >= 3:
                            weigh_values(done[0], done[1], done[2])
                        if i == LAG % SLOTS and one:
                            weigh_values(*one, 0)
                        if i == 1 and (not known(p) or p + 1 < PAIRS):
                            pe.wait_ge(wq_split, p + 2)
                            if any_step(p, b, 2):
                                pe.wait_ge(wide_ok, ordinal(p, b) - 1)
                            else:
                                pe.wait_ge(qlo_ok[1], 1)
                            queries(p + 1, b, 1 - par, X_BANK)
                        if i == 2 and two:
                            project(*two)
                        if i == 3 and one:
                            if not known(p) or p + 1 < PAIRS:
                                pe.wait_ge(qlo_ok[b], p + 2)
                            else:
                                pe.wait_ge(wide_ok, ordinal(p, b) - 1)
                            inverseT(*one)
                        if i == 4 and one:
                            inverse_wide(*one)
                        if known(p) and p == 0 and b == 1:
                            if i == 1:
                                pe.wait_ge(place_ok, 2)
                                pe.wait_ge(ld["wo"], 16)
                                for a in range(PAIRS):
                                    last = mm(bank[6][0:H, 0:C], place_v[:, a * H:(a + 1) * H], wo_sb[:, a * C:(a + 1) * C],
                                              a == 0, a == PAIRS - 1)
                                last.then_inc(nout_ps, 1)
                            if i == 4:
                                pe.wait_ge(nout_ok, 1)
                                for n in range(B):
                                    mm(F_BANK[n][:], zero_bf[:, 0:P], zero_bf[:], True, False, loose=True).then_inc(fin_zero, 1)
                        if known(p) and p == PAIRS and i == 0:
                            pe.wait_ge(nullp_ok, B * PAIRS - B + b + 1)
                            pe.wait_ge(neg_ok, NU * B * PAIRS)
                            for u in range(QT):
                                last = nc.tensor.transpose(S_BANK[b][0:H, cols(u)], null_prob[:, b * QT + u, :], ident[:])
                            last.then_inc(npT_ps, 1)
                        if known(p) and p == PAIRS and i == 2:
                            pe.wait_ge(npT_ok, b + 1)
                            for u in range(QT):
                                last = mm(F_BANK[b][:, cols(u)], null_probT[:, cols(b * QT + u)], null_out[:],
                                          False, u == QT - 1, loose=True)
                            last.then_inc(fin_ps, 1)

            loop(nc.tensor, body)


_INS = ["x", "cond_64", "fside_16xSxS_0", "mask_BxS_bk0", "L0_cond_wt", "L0_cond_wg", "L0_cond_w_gate", "L0_cond_w_up",
        "L0_cond_w_down", "L0_cond_sw_gate", "L0_cond_sw_up", "L0_cond_sw_down", "L1_cond_g_in",
        "L1_cond_null_attn_bias", "L1_cond_Wq", "L1_cond_Wkv", "L1_cond_Wo", "L1_cond_g_out"]


def kernel(**inputs):
    import numpy as np
    import concourse.bacc as bacc
    from concourse.bass_utils import run_bass_kernel_spmd as run

    nc = bacc.Bacc("TRN2", target_bir_lowering=False, num_devices=1)
    arrays, args = {}, []
    for name in _INS:
        a = np.ascontiguousarray(inputs[name])
        arrays[name + "_dram"] = a
        args.append(nc.dram_tensor(name + "_dram", a.shape, mybir.dt.from_np(a.dtype), kind="ExternalInput").ap())
    x = inputs["x"]
    args.append(nc.dram_tensor("out_dram", tuple(x.shape), mybir.dt.float32, kind="ExternalOutput").ap())
    moe_then_attention_program(nc, *args)
    r = run(nc, [arrays], core_ids=[0])
    return r.results[0]["out_dram"]
```

```python
import concourse.bass as bass
from concourse import mybir
from contextlib import ExitStack


def moe_then_attention_program(nc, x, cond, score_bias, keep_mask, wt, wg, w_gate, w_up, w_down,
                               sw_gate, sw_up, sw_down, g_in, null_bias, w_q, w_kv, w_o, g_out, out):
    f32, f32r, u8 = mybir.dt.float32, mybir.dt.float32r, mybir.dt.uint8
    bf16 = mybir.dt.bfloat16
    ALU, ACT, AX = mybir.AluOpType, mybir.ActivationFunctionType, mybir.AxisListType

    P = 128
    B, S, C = x.shape
    E, G = wg.shape
    M = w_gate.shape[2]
    H = null_bias.shape[0]
    D = w_kv.shape[1] // 2
    QT = S // P
    U = B * QT
    T = B * S
    PAIRS = H // 2
    EP = E // 2
    NM = EP + 1
    SHARED = EP
    WARM = 7
    NEG = -1.0e30
    EPS = 1e-5
    SLOPE = 0.01

    UNITS = [[(0, 3, 0)], [(0, 2, 0), (0, 0, 3 * P)], [(0, 1, 0), (1, 1, 2 * P)],
             [(1, 3, 0)], [(1, 2, 0), (1, 0, 3 * P)]]
    SLOTS = len(UNITS)
    before = [sum(len(v) for v in UNITS[:i]) for i in range(SLOTS + 1)]
    NU = before[SLOTS]
    TRI = P * QT * (QT + 1) // 2
    at_t = [7 * P, 8 * P, 4 * P, 0]
    at_j = [0, 4 * P, 8 * P, 7 * P]
    BLOCKS = [[(0, t, 0) for t in range(4)], [(0, t, 1) for t in (1, 2, 3)] + [(0, 3, 3)],
              [(1, t, 0) for t in range(4)], [(1, t, 1) for t in (1, 2, 3)] + [(1, 3, 3)],
              [(h, t, 2) for h in range(2) for t in (2, 3)]]
    PIECES = [([0], (0, 2)), ([1, 3], (1, 3)), ([2], (4,))]
    LAG = 4
    R = 2 * QT

    ctx = ExitStack()
    with ctx:
        def sb(name, shape, dt=f32):
            return ctx.enter_context(nc.sbuf_tensor(name, shape, dt))

        def sem(name):
            return ctx.enter_context(nc.semaphore(name))

        x_sb = sb("x_sb", [P, U, C])
        wt_sb = sb("wt_sb", [E, C])
        wg_sb = sb("wg_sb", [E, G])
        cond_sb = sb("cond_sb", [B, G])
        gate_sb = sb("gate_sb", [P, NM, P])
        up_sb = sb("up_sb", [P, NM, P])
        down_sb = sb("down_sb", [P, NM, C])
        wq_sb = sb("wq_sb", [P, PAIRS * P])
        wkv_sb = sb("wkv_sb", [P, 2 * D])
        wo_sb = sb("wo_sb", [P, PAIRS * C])
        g_in_col = sb("g_in_col", [P, 1])
        g_out_row = sb("g_out_row", [P, C])
        null_bias_row = sb("null_bias_row", [P, H])
        null_k_row = sb("null_k_row", [P, D])
        null_v_col = sb("null_v_col", [P, 1])
        keep_row = sb("keep_row", [D + 1, T], u8)
        bias_sb = sb("bias_sb", [P, 2, 2, TRI])

        ident = sb("ident", [P, P])
        earlier = sb("earlier", [P, E, E])
        pick = sb("pick", [32 + E, EP, P])
        pick_r = sb("pick_r", [32 + E, EP, P], f32r)
        row_of = sb("row_of", [2 * R, QT, P])
        row_of_r = sb("row_of_r", [2 * R, QT, P], f32r)
        minus_half = sb("minus_half", [P, QT])
        zero_bf = sb("zero_bf", [P, S], bf16)
        place_v = sb("place_v", [P, PAIRS * H])

        xT = sb("xT", [P, T])
        wtT = sb("wtT", [P, E])
        wgT = sb("wgT", [G, E])
        condT = sb("condT", [G, B, P])
        top = sb("top", [P, U])
        logit = sb("logit", [P, U, E])
        expo = sb("expo", [P, U, E])
        total = sb("total", [P, U])
        score = sb("score", [P, U, E])
        ahead_by = sb("ahead_by", [P, U, E * E])
        ahead = sb("ahead", [P, U, E * E])
        rank = sb("rank", [P, U, E])
        chosen = sb("chosen", [P, U, E])
        weight = sb("weight", [P, U, E])
        weightT = sb("weightT", [32 + E, T], f32r)
        gate = sb("gate", [P, 2, S])
        sloped = sb("sloped", [P, 2, S])
        leaky = sb("leaky", [P, 2, S])
        hidden = sb("hidden", [P, NM, T])
        x1 = sb("x1", [P, U, C])

        stats = sb("stats", [P, U, 6])
        moments = sb("moments", [P, U, 2])
        var_eps = sb("var_eps", [P, U])
        rstd = sb("rstd", [P, U])
        xn = sb("xn", [P, U, C])
        xnT_hi = sb("xnT_hi", [P, T], f32r)
        xnT_lo = sb("xnT_lo", [P, T], f32r)

        VW = D + H
        vw = sb("vw", [P, VW])
        null_prod = sb("null_prod", [P, H * D])
        wk_hi = sb("wk_hi", [P, P], f32r)
        wk_lo = sb("wk_lo", [P, P], f32r)
        vw_hi = sb("vw_hi", [P, VW], f32r)
        vw_lo = sb("vw_lo", [P, VW], f32r)
        wq_hi = sb("wq_hi", [P, 2, P], f32r)
        wq_lo = sb("wq_lo", [P, 2, P], f32r)
        first_w_hi = sb("first_w_hi", [P, 2, 2, D], f32r)
        first_w_lo = sb("first_w_lo", [P, 2, 2, D], f32r)
        k_hi = sb("k_hi", [P, T], f32r)
        k_lo = sb("k_lo", [D + 1, T], f32r)
        v_sb = sb("v_sb", [P, U, D])
        neg_null = sb("neg_null", [P, B, H, QT])
        neg_null_now = sb("neg_null_now", [P, B, R])

        q_hi = sb("q_hi", [P, T], f32r)
        q_lo = sb("q_lo", [P, T], f32r)
        q_both = [sb(f"q_both{h}", [P, T], f32r) for h in range(2)]
        q_one = [sb(f"q_one{h}", [D + 1, T], f32r) for h in range(2)]

        neg_s = sb("neg_s", [P, 2, S])
        probs = hidden[:].rearrange("p m t -> p (m t)").rearrange("p (b h c) -> p b h c", b=B, h=2)
        probsT = sb("probsT", [P, B, 2, TRI])
        up_lo_sb = sb("up_lo_sb", [P, NM * P], f32r)
        gate_hi, gate_lo, up_hi, up_lo = (a[:, 0:NM * P].rearrange("p (m c) -> p m c", m=NM)
                                          for a in (q_both[0], q_both[1], k_hi, up_lo_sb))
        xT_hi, xT_lo = q_hi, q_lo
        neg_max = sb("neg_max", [P, B, R])
        row_sum = sb("row_sum", [P, B, R])
        null_gap = sb("null_gap", [P, B, R])
        null_exp = sb("null_exp", [P, B, R])
        full_sum = sb("full_sum", [P, B, R])
        inv_sum = sb("inv_sum", [P, B, R])
        inv_split = sb("inv_split", [P, B, 2 * R], f32r)
        inv_T = sb("inv_T", [2 * R, B, P], f32r)
        inv_wide = sb("inv_wide", [P, B, S])
        null_prob = sb("null_prob", [P, U, H])
        headsT = sb("headsT", [P, T])
        null_out = sb("null_out", [H, C])
        null_probT = sb("null_probT", [H, T])
        normed, result = xn, x_sb

        bank = [ctx.enter_context(nc.psum_tensor(f"bank{i}", [P, S], f32)) for i in range(8)]
        S_BANK, T_BANK, PV_BANK, X_BANK, F_BANK = bank[0:2], bank[2:4], bank[4], bank[5], bank[6:8]
        FIRST_BANK = [[bank[5], bank[4]], [bank[4], bank[6]]]
        GATE_BANK, UP_BANK, Y_BANK, W_BANK = bank[0:2], bank[2:4], bank[4:8], bank[6:8]

        ld = {n: sem("ld_" + n) for n in ("x", "router", "gate", "up", "down", "sgate", "sup", "sdown",
                                          "wq", "wkv", "wo", "norm", "null", "null_v", "mask")}
        bias_ld = [sem("bias_ld_even"), sem("bias_ld_odd")]
        def sems(names, n=None):
            return [sem(x) if n is None else [sem(f"{x}_{i}") for i in range(n)] for x in names.split()]

        const_step, ident_ok, earlier_ok, pick_ok, row_of_ok = sems("const_step ident_ok earlier_ok pick_ok row_of_ok")
        leaky_ok, vw_step, wkv_split_ok, null_prod_ok = sems("leaky_ok vw_step wkv_split_ok null_prod_ok")
        wq_hi_ok, wq_split, rstd_ok, gap_ok, sum_ok = sems("wq_hi_ok wq_split rstd_ok gap_ok sum_ok")
        inv_hi_ok, inv_split_ok, nullp_ok = sems("inv_hi_ok inv_split_ok nullp_ok")
        bias_ok, null_now_ok = sems("bias_ok null_now_ok", 2)
        xT_ps, small_ps, logit_ps, gate_ps, up_ps, wT_ps, wb_ps, y_ps = sems("xT_ps small_ps logit_ps gate_ps up_ps wT_ps wb_ps y_ps")
        xnT_ps, k_ps, v_ps, nout_ps, fin_zero = sems("xnT_ps k_ps v_ps nout_ps fin_zero")
        s_ps, t_ps, pv_ps, invT_ps, wide_ps, wo_ps, npT_ps, null_ps = sems("s_ps t_ps pv_ps invT_ps wide_ps wo_ps npT_ps null_ps")
        xT_a, expo_ok, sloped_ok, wTh_ok, xnTh_ok, kh_ok = sems("xT_a expo_ok sloped_ok wTh_ok xnTh_ok kh_ok")
        exp_ok, evac_a, nexp_ok, invT_ok, wide_ok, npT_ok = sems("exp_ok evac_a nexp_ok invT_ok wide_ok npT_ok")
        dve_step, warm_ok, zero_ok, xT_v, small_ok, logit_ok, weight_ok = sems("dve_step warm_ok zero_ok xT_v small_ok logit_ok weight_ok")
        t1_ok, h_ok, wTl_ok, x1_ok, var_ok, xn_ok, xnTl_ok = sems("t1_ok h_ok wTl_ok x1_ok var_ok xn_ok xnTl_ok")
        wn_ok, kl_ok, v_ok, negnull_ok, mask_ok, place_ok = sems("wn_ok kl_ok v_ok negnull_ok mask_ok place_ok")
        neg_ok, evac_v, inv_ok, head_ok, nout_ok, result_ok = sems("neg_ok evac_v inv_ok head_ok nout_ok result_ok")
        q_ps, qhi_ok, qlo_ok, q_ok = sems("q_ps qhi_ok qlo_ok q_ok", B)
        x_hi_ok, w_hi_ok, x_lo_ok, w_lo_ok = sems("x_hi_ok w_hi_ok x_lo_ok w_lo_ok")
        first_w_ok, first_ps, first_hi, first_one, first_lo = sems("first_w_ok first_ps first_hi first_one first_lo")
        stored = sem("stored")
        dve_passed, pool_passed = sems("dve_passed pool_passed")

        tiles = lambda a: a.rearrange("b (t p) c -> p (b t) c", p=P)
        bias_view = score_bias.rearrange("h (t p) j -> p h t j", p=P)
        cols = lambda u: slice(u * P, (u + 1) * P)
        half = lambda n: slice(n * S, (n + 1) * S)

        STEPS = [(m, n) for n in range(B) for m in [SHARED] + list(range(EP))]
        WEIGHTED = [s for s, (m, n) in enumerate(STEPS) if m != SHARED]

        def stand_alone(engine, passed):
            engine.sem_inc(passed, 1)

        def known(p):
            return isinstance(p, int)

        def back(p, b, steps):
            q, c = p - (steps + 1 - b) // 2, (b + steps) % 2
            return None if known(p) and not 0 <= q < PAIRS else (q, c)

        def lagged(p, b, i, slots):
            d = (slots - i + SLOTS - 1) // SLOTS
            step = back(p, b, d)
            return None if step is None else (*step, i - slots + d * SLOTS)

        def ordinal(p, b):
            return B * p + b

        def any_step(p, b, least):
            return not known(p) or ordinal(p, b) >= least

        def evacuated(engine, p, b, i):
            g = SLOTS * b + i
            engine.wait_ge(evac_v if g % 2 else evac_a, SLOTS * p + g // 2 + 1)

        def evacuate(engine, p, b, i):
            n = ordinal(p, b)
            engine.wait_ge(t_ps, SLOTS * n + i + 1)
            if i < 2 and any_step(p, b, 2):
                engine.wait_ge(pv_ps, len(PIECES) * n - len(PIECES))
            par = (b + i) % 2
            if i == SLOTS - 1:
                to = probsT[:, b, :, at_j[2]:at_j[2] + 2 * P]
                src = T_BANK[par][:].rearrange("p (h c) -> p h c", h=2)
            else:
                to = probsT[:, b, i // 2, (i % 2) * S:(i % 2 + 1) * S]
                src = T_BANK[par][:]
            if par == 0:
                nc.scalar.activation(to, src, ACT.Copy).then_inc(evac_a, 1)
            else:
                nc.vector.tensor_copy(to, src).then_inc(evac_v, 1)

        def loop(engine, body, ahead=0):
            body(0, 0, 0)
            with engine.Fori(1, PAIRS // 2 - ahead) as turn:
                body(2 * turn - 1, 1, turn - 1)
                body(2 * turn, 0, turn)
            for p in range(PAIRS - 1 - 2 * ahead, PAIRS + 1):
                body(p, p % 2, p // 2)

        block = ctx.enter_context(nc.Block())

        @block.sync
        def _(sp):
            sp.dma_start(x_sb[:], tiles(x)).then_inc(ld["x"], 16)
            sp.dma_start(wt_sb[:], wt).then_inc(ld["router"], 16)
            sp.dma_start(wg_sb[:], wg).then_inc(ld["router"], 16)
            sp.dma_start(cond_sb[:], cond).then_inc(ld["router"], 16)
            sp.dma_start(gate_sb[:, SHARED, :], sw_gate).then_inc(ld["sgate"], 16)
            sp.dma_start(up_sb[:, SHARED, :], sw_up).then_inc(ld["sup"], 16)
            sp.dma_start(gate_sb[:, 0:EP, :].rearrange("c e (k m) -> c (e k) m", k=2),
                         w_gate.rearrange("e c m -> c e m")).then_inc(ld["gate"], 16)
            sp.dma_start(up_sb[:, 0:EP, :].rearrange("c e (k m) -> c (e k) m", k=2),
                         w_up.rearrange("e c m -> c e m")).then_inc(ld["up"], 16)
            sp.dma_start(wkv_sb[:], w_kv).then_inc(ld["wkv"], 16)
            sp.dma_start(wq_sb[:], w_q).then_inc(ld["wq"], 16)
            sp.dma_start(null_k_row[:], cond[0:1, :].broadcast_to([P, D])).then_inc(ld["null"], 16)
            sp.dma_start(null_bias_row[:], null_bias.rearrange("(a h) -> a h", a=1).broadcast_to([P, H])).then_inc(ld["null"], 16)
            sp.dma_start(down_sb[:, SHARED, :], sw_down).then_inc(ld["sdown"], 16)
            sp.dma_start(down_sb[:, 0:EP, :], w_down.rearrange("(e k) m c -> (k m) e c", k=2)).then_inc(ld["down"], 16)
            sp.dma_start(keep_row[D:D + 1, :], keep_mask.rearrange("(a b) s -> a (b s)", a=1)).then_inc(ld["mask"], 16)
            sp.dma_start(g_in_col[:], g_in.rearrange("(c a) -> c a", a=1)).then_inc(ld["norm"], 16)
            sp.dma_start(g_out_row[:], g_out.rearrange("(a c) -> a c", a=1).broadcast_to([P, C])).then_inc(ld["norm"], 16)
            for k in range(2):
                sp.dma_start(null_v_col[k * D:(k + 1) * D, :], cond[1:2, :].rearrange("a d -> d a")).then_inc(ld["null_v"], 16)

            def load_bias(p, par):
                for t in range(QT):
                    w = (t + 1) * P
                    sp.dma_start(bias_sb[:, par, :, at_t[t]:at_t[t] + w],
                                 bias_view[:, bass.ds(2 * p, 2), t, 0:w]).then_inc(bias_ld[par], 16)

            def copy_queries(p, b):
                sp.wait_ge(qhi_ok[b], p)
                sp.wait_ge(qlo_ok[b], p)
                sp.wait_ge(s_ps, SLOTS * ordinal(p - 1, b) + SLOTS)
                for h in range(2):
                    own = slice(h * D, (h + 1) * D)
                    for to, rows, part in ((q_both[h], slice(0, D), q_hi), (q_both[h], slice(D, P), q_lo),
                                           (q_one[h], slice(0, D), q_hi)):
                        sp.dma_start(to[rows, half(b)].bitcast(f32), part[own, half(b)].bitcast(f32)).then_inc(q_ok[b], 16)

            load_bias(0, 0)
            sp.dma_start(wo_sb[:].rearrange("p (a c) -> p a c", c=C), w_o.rearrange("(a p) c -> p a c", p=P)).then_inc(ld["wo"], 16)
            load_bias(1, 1)

            def body(p, par, j):
                if known(p) and p + 1 >= PAIRS:
                    return
                for b in range(B):
                    copy_queries(p + 1, b)
                if not known(p) or p + 2 < PAIRS:
                    sp.wait_ge(neg_ok, NU * ordinal(p, B - 1) + NU)
                    load_bias(p + 2, par)

            loop(nc.sync, body, ahead=1)
            for n in range(B):
                for k in range(2):
                    own = slice(n * QT + k * QT // 2, n * QT + (k + 1) * QT // 2)
                    sp.wait_ge(result_ok, 2 * n + k + 1)
                    sp.dma_start(tiles(out)[:, own, :], result[:, own, :]).then_inc(stored, 16)
            sp.wait_ge(stored, 32 * B)

        @block.gpsimd
        def _(pool):
            steps = [0]

            def step(ins):
                steps[0] += 1
                ins.then_inc(const_step, 1)
                pool.wait_ge(const_step, steps[0])

            step(pool.memset(ident[:], 0.0))
            pool.affine_select(out=ident[:], in_=ident[:], compare_op=ALU.not_equal, fill=1.0, base=0,
                               pattern=[[-1, P]], channel_multiplier=1).then_inc(ident_ok, 1)
            step(pool.memset(earlier[:], 1.0))
            pool.affine_select(out=earlier[:], in_=earlier[:], compare_op=ALU.is_gt, fill=0.0, base=0,
                               pattern=[[1, E], [-1, E]], channel_multiplier=0).then_inc(earlier_ok, 1)
            step(pool.memset(pick[:], 0.0))
            for base in (0, -32):
                step(pool.affine_select(out=pick[:], in_=pick[:], compare_op=ALU.not_equal, fill=1.0, base=base,
                                        pattern=[[-2, EP], [-1, 2], [0, M]], channel_multiplier=1))
            pool.tensor_copy(pick_r[:], pick[:]).then_inc(pick_ok, 1)

            def leaky_step(s):
                pool.wait_ge(sloped_ok, s + 1)
                if s >= 2:
                    pool.wait_ge(t1_ok, s - 1)
                pool.tensor_tensor(leaky[:, s % 2, :], gate[:, s % 2, :], sloped[:, s % 2, :], ALU.subtract).then_inc(leaky_ok, 1)

            def split_wq(p, par):
                own = wq_sb[:, bass.ds(p * P, P)]
                pool.tensor_copy(wq_hi[:, par, :], own).then_inc(wq_hi_ok, 1)
                pool.wait_ge(wq_hi_ok, p)
                stand_alone(pool, pool_passed)
                pool.tensor_tensor(wq_lo[:, par, :], own, wq_hi[:, par, :].bitcast(f32), ALU.subtract).then_inc(wq_split, 1)

            def causal(par, j):
                pool.wait_ge(bias_ld[par], 16 * QT * j + 16 * QT)
                stand_alone(pool, pool_passed)
                for t in range(QT):
                    at = at_t[t] + t * P
                    diagonal = bias_sb[:, par, :, at:at + P]
                    pool.affine_select(out=diagonal, in_=diagonal, compare_op=ALU.is_ge, fill=NEG, base=0,
                                       pattern=[[0, 2], [-1, P]], channel_multiplier=1).then_inc(bias_ok[par], 1)

            def rstd_of(count, own):
                pool.wait_ge(var_ok, count)
                pool.tensor_tensor(rstd[:, own], var_eps[:, own], minus_half[:, 0:own.stop - own.start], ALU.pow).then_inc(rstd_ok, 1)

            pool.wait_ge(ld["wkv"], 16)
            for k in range(2):
                pool.tensor_copy(wk_hi[:, k * D:(k + 1) * D], wkv_sb[:, 0:D]).then_inc(vw_step, 1)
            pool.tensor_copy(vw[:, 0:D], wkv_sb[:, D:2 * D]).then_inc(vw_step, 1)
            pool.wait_ge(vw_step, 2)
            for k in range(2):
                pool.tensor_tensor(wk_lo[:, k * D:(k + 1) * D], wkv_sb[:, 0:D],
                                   wk_hi[:, k * D:(k + 1) * D].bitcast(f32), ALU.subtract).then_inc(wkv_split_ok, 1)
            leaky_step(0)
            pool.wait_ge(ld["wq"], 16)
            pool.wait_ge(ld["null"], 32)
            pool.tensor_tensor(null_prod[:].rearrange("p (h d) -> p h d", d=D), wq_sb[:].rearrange("p (h d) -> p h d", d=D),
                               null_k_row[:].unsqueeze(1).broadcast_to([P, H, D]), ALU.mult).then_inc(null_prod_ok, 1)
            for s in range(1, 4):
                leaky_step(s)
            first = wq_sb[:, 0:P].rearrange("p (h d) -> p h d", d=D)
            for k in range(2):
                pool.tensor_copy(first_w_hi[:, :, k, :], first).then_inc(vw_step, 1)
            pool.wait_ge(vw_step, 5)
            for k in range(2):
                pool.tensor_tensor(first_w_lo[:, :, k, :], first, first_w_hi[:, :, k, :].bitcast(f32), ALU.subtract).then_inc(first_w_ok, 1)
            leaky_step(4)
            leaky_step(5)
            pool.wait_ge(wn_ok, 1)
            pool.wait_ge(vw_step, 3)
            pool.tensor_copy(vw_hi[:], vw[:]).then_inc(vw_step, 1)
            leaky_step(6)
            pool.wait_ge(vw_step, 6)
            pool.tensor_tensor(vw_lo[:], vw[:], vw_hi[:].bitcast(f32), ALU.subtract).then_inc(wkv_split_ok, 1)
            for q in range(2):
                rstd_of(q + 1, slice(q * QT // 2, (q + 1) * QT // 2))
            for s in range(7, len(STEPS)):
                leaky_step(s)
            split_wq(1, 1)
            step(pool.memset(row_of[:], 0.0))
            for base in (0, -R):
                step(pool.affine_select(out=row_of[:], in_=row_of[:], compare_op=ALU.not_equal, fill=1.0, base=base,
                                        pattern=[[-1, QT], [-QT, 2], [0, D]], channel_multiplier=1))
            causal(0, 0)

            def first_null(n):
                pool.wait_ge(negnull_ok, n + 1)
                pool.tensor_copy(neg_null_now[:, n, :].rearrange("p (h t) -> p h t", h=2),
                                 neg_null[:, n, 0:2, :]).then_inc(null_now_ok[n], 1)

            rstd_of(3, slice(QT, QT + QT // 2))
            first_null(0)
            rstd_of(4, slice(QT + QT // 2, U))
            pool.tensor_copy(row_of_r[:], row_of[:]).then_inc(row_of_ok, 1)
            first_null(1)

            def inverses(p, b):
                n = ordinal(p, b)
                pool.wait_ge(neg_ok, NU * n + NU)
                pool.tensor_tensor(null_gap[:, b, :], neg_max[:, b, :], neg_null_now[:, b, :], ALU.subtract).then_inc(gap_ok, 1)
                if not known(p) or p + 1 < PAIRS:
                    pool.wait_ge(gap_ok, n + 1)
                    stand_alone(pool, pool_passed)
                    pool.tensor_copy(neg_null_now[:, b, :].rearrange("p (h t) -> p h t", h=2),
                                     neg_null[:, b, bass.ds(2 * p + 2, 2), :]).then_inc(null_now_ok[b], 1)
                pool.wait_ge(nexp_ok, n + 1)
                pool.tensor_tensor(full_sum[:, b, :], row_sum[:, b, :], null_exp[:, b, :], ALU.add).then_inc(sum_ok, 1)
                pool.wait_ge(inv_ok, n + 1)
                stand_alone(pool, pool_passed)
                pool.tensor_copy(inv_split[:, b, 0:R], inv_sum[:, b, :]).then_inc(inv_hi_ok, 1)
                pool.wait_ge(inv_hi_ok, n + 1)
                pool.tensor_tensor(inv_split[:, b, R:2 * R], inv_sum[:, b, :], inv_split[:, b, 0:R].bitcast(f32),
                                   ALU.subtract).then_inc(inv_split_ok, 1)
                pool.tensor_tensor(null_prob[:, b * QT:(b + 1) * QT, bass.ds(2 * p, 2)].rearrange("p t h -> p h t"),
                                   null_exp[:, b, :].rearrange("p (h t) -> p h t", h=2),
                                   inv_sum[:, b, :].rearrange("p (h t) -> p h t", h=2), ALU.mult).then_inc(nullp_ok, 1)

            def body(p, par, j):
                if known(p) and p == PAIRS:
                    return
                if not known(p) or p + 1 < PAIRS:
                    causal(1 - par, j + par)
                if not known(p) or p + 2 < PAIRS:
                    if not known(p) or p > 0:
                        pool.wait_ge(q_ps[B - 1], p)
                        stand_alone(pool, pool_passed)
                    split_wq(p + 2, par)
                for b in range(B):
                    inverses(p, b)

            loop(nc.gpsimd, body, ahead=1)
            for n in range(B):
                rstd_of(2 * B + n + 1, slice(n * QT, (n + 1) * QT))

        @block.scalar
        def _(act):
            act.wait_ge(xT_ps, 1)
            nc.scalar.activation(xT[:, half(0)], bank[0][:], ACT.Copy).then_inc(xT_a, 1)
            for n, made in ((0, xT_a), (1, xT_v)):
                act.wait_ge(made, 1)
                nc.scalar.activation(xT_hi[:, half(n)], xT[:, half(n)], ACT.Copy).then_inc(x_hi_ok, 1)

            def gate_step(s):
                act.wait_ge(gate_ps, s + 1)
                if s >= 2:
                    act.wait_ge(leaky_ok, s - 1)
                nc.scalar.activation(gate[:, s % 2, :], GATE_BANK[s % 2][:], ACT.Relu)
                nc.scalar.activation(sloped[:, s % 2, :], GATE_BANK[s % 2][:], ACT.Relu, scale=-SLOPE).then_inc(sloped_ok, 1)

            gate_step(0)
            for hi, w, kinds in ((gate_hi, gate_sb, ("sgate", "gate")), (up_hi, up_sb, ("sup", "up"))):
                for k in kinds:
                    act.wait_ge(ld[k], 16)
                nc.scalar.activation(hi, w[:], ACT.Copy).then_inc(w_hi_ok, 1)
            act.wait_ge(logit_ok, 1)
            nc.scalar.activation(expo[:], logit[:], ACT.Exp, scale=0.5).then_inc(expo_ok, 1)

            def tokens_hi(n, psum):
                act.wait_ge(xnT_ps, n + 1)
                nc.scalar.activation(xnT_hi[:, half(n)], psum[:], ACT.Copy, scale=g_in_col[:, 0:1]).then_inc(xnTh_ok, 1)

            def keys_hi(n, psum):
                act.wait_ge(k_ps, n + 1)
                nc.scalar.activation(k_hi[:, half(n)], psum[:], ACT.Copy).then_inc(kh_ok, 1)

            def queries_hi(p, b, psum):
                act.wait_ge(q_ps[b], p)
                if not known(p) or p > 1:
                    act.wait_ge(q_ok[b], 96 * p - 96)
                nc.scalar.activation(q_hi[:, half(b)], psum[:], ACT.Copy, scale=float(D) ** -0.5).then_inc(qhi_ok[b], 1)

            def first_queries_hi(b):
                for h in range(2):
                    act.wait_ge(first_ps, 2 * b + h + 1)
                    nc.scalar.activation(q_both[h][:, half(b)], FIRST_BANK[b][h][:], ACT.Copy,
                                         scale=float(D) ** -0.5).then_inc(first_hi, 1)
                    nc.scalar.activation(q_one[h][0:D, half(b)], FIRST_BANK[b][h][0:D, :], ACT.Copy,
                                         scale=float(D) ** -0.5).then_inc(first_one, 1)

            for s in range(1, len(STEPS)):
                if s == 4:
                    for n in range(B):
                        act.wait_ge(wT_ps, n + 1)
                        nc.scalar.activation(weightT[0:E, half(n)], W_BANK[n][0:E, :], ACT.Copy).then_inc(wTh_ok, 1)
                gate_step(s)
                if s == 8:
                    act.wait_ge(ld["norm"], 32)
                    tokens_hi(0, bank[4])
            first_queries_hi(0)
            keys_hi(0, bank[0])

            def exp_slot(p, b, i):
                n = ordinal(p, b)
                for at, (h, t, off) in enumerate(UNITS[i]):
                    w = (t + 1) * P
                    act.wait_ge(neg_ok, NU * n + before[i] + at + 1)
                    if i == 0 and any_step(p, b, 2):
                        act.wait_ge(t_ps, SLOTS * n - SLOTS)
                    nc.scalar.activation(probs[:, b, h, at_t[t]:at_t[t] + w], neg_s[:, (b + i) % 2, off:off + w], ACT.Exp,
                                         bias=neg_max[:, b, h * QT + t:h * QT + t + 1], scale=-1.0,
                                         accum_out=row_sum[:, b, h * QT + t:h * QT + t + 1]).then_inc(exp_ok, 1)

            def body(p, par, j):
                for b in range(B):
                    for i in range(SLOTS):
                        last, two = back(p, b, 1), back(p, b, 2)
                        if last and i == 4:
                            act.wait_ge(invT_ps, ordinal(*last) + 1)
                            nc.scalar.activation(inv_T[:, last[1], :], X_BANK[0:2 * R, 0:P], ACT.Copy).then_inc(invT_ok, 1)
                        if two and i == 0:
                            act.wait_ge(wide_ps, ordinal(*two) + 1)
                            nc.scalar.activation(inv_wide[:, two[1], :], X_BANK[:], ACT.Copy).then_inc(wide_ok, 1)
                        if i == 2 and (not known(p) or p + 1 < PAIRS):
                            queries_hi(p + 1, b, X_BANK)
                        if known(p) and (p, b) == (0, 0):
                            if i == 1:
                                tokens_hi(1, bank[3])
                            if i == 2:
                                keys_hi(1, bank[2])
                            if i == 3:
                                first_queries_hi(1)
                        done = lagged(p, b, i, LAG)
                        if done and (done[1] + done[2]) % 2 == 0:
                            evacuate(act, *done)
                        if not known(p) or p < PAIRS:
                            exp_slot(p, b, i)
                        if last and i == 0:
                            act.wait_ge(gap_ok, ordinal(*last) + 1)
                            nc.scalar.activation(null_exp[:, last[1], :], null_gap[:, last[1], :], ACT.Exp).then_inc(nexp_ok, 1)
                        if known(p) and p == PAIRS and (b, i) in ((0, 2), (1, 0)):
                            act.wait_ge(npT_ps, b + 1)
                            nc.scalar.activation(null_probT[:, half(b)], S_BANK[b][0:H, :], ACT.Copy).then_inc(npT_ok, 1)

            loop(nc.scalar, body)

        @block.vector
        def _(dve):
            steps = [0]

            def step(ins):
                steps[0] += 1
                ins.then_inc(dve_step, 1)
                dve.wait_ge(dve_step, steps[0])

            nc.vector.memset(zero_bf[:].bitcast(f32), 0.0).then_inc(warm_ok, 1)
            nc.vector.memset(minus_half[:], -0.5)
            nc.vector.memset(place_v[:], 0.0)
            for h in range(2):
                nc.vector.memset(q_one[h][D:D + 1, :].bitcast(f32), 1.0).then_inc(zero_ok, 1)
            step(nc.vector.memset(weightT[:].bitcast(f32), 0.0))
            dve.wait_ge(xT_ps, 2)
            nc.vector.tensor_copy(xT[:, half(1)], bank[1][:]).then_inc(xT_v, 1)
            dve.wait_ge(small_ps, 1)
            nc.vector.tensor_copy(wtT[:], bank[2][:, 0:E])
            nc.vector.tensor_copy(wgT[:], bank[2][0:G, E:2 * E])
            nc.vector.tensor_copy(condT[:], bank[2][0:G, 2 * E:2 * E + B].unsqueeze(2).broadcast_to([G, B, P])).then_inc(small_ok, 1)

            for n in range(B):
                dve.wait_ge(x_hi_ok, n + 1)
                dve.wait_ge(xT_a if n == 0 else xT_v, 1)
                nc.vector.tensor_tensor(xT_lo[:, half(n)], xT[:, half(n)], xT_hi[:, half(n)].bitcast(f32),
                                        ALU.subtract).then_inc(x_lo_ok, 1)
            dve.wait_ge(w_hi_ok, 1)
            nc.vector.tensor_tensor(gate_lo, gate_sb[:], gate_hi.bitcast(f32), ALU.subtract).then_inc(w_lo_ok, 1)

            dve.wait_ge(logit_ps, 1)
            wide = lambda a: a.unsqueeze(2).broadcast_to([*a.shape, E])
            logits = [Y_BANK[n][:, 0:QT * E].rearrange("p (u e) -> p u e", e=E) for n in range(B)]
            own = [slice(n * QT, (n + 1) * QT) for n in range(B)]
            for n in range(B):
                last = nc.vector.reduce_max(top[:, own[n]], logits[n], AX.X)
            step(last)
            for n in range(B):
                last = nc.vector.tensor_tensor(logit[:, own[n], :], logits[n], wide(top[:, own[n]]), ALU.subtract)
            last.then_inc(logit_ok, 1)
            dve.wait_ge(w_hi_ok, 2)
            nc.vector.tensor_tensor(up_lo, up_sb[:], up_hi.bitcast(f32), ALU.subtract).then_inc(w_lo_ok, 1)

            def t1_step(s):
                m, n = STEPS[s]
                dve.wait_ge(leaky_ok, s + 1)
                dve.wait_ge(up_ps, s + 1)
                ins = nc.vector.tensor_tensor(hidden[:, m, half(n)], leaky[:, s % 2, :], UP_BANK[s % 2][:], ALU.mult)
                ins.then_inc(t1_ok, 1)

            t1_step(0)
            dve.wait_ge(expo_ok, 1)
            step(nc.vector.reduce_sum(total[:], expo[:], AX.X))
            step(nc.vector.reciprocal(total[:], total[:]))
            step(nc.vector.tensor_tensor(score[:], expo[:], wide(total[:]), ALU.mult))
            other = lambda a: a.unsqueeze(2).broadcast_to([P, U, E, E])
            own = lambda a: a.unsqueeze(3).broadcast_to([P, U, E, E])
            four = lambda a: a.rearrange("p u (e f) -> p u e f", f=E)
            step(nc.vector.tensor_tensor(four(ahead_by[:]), other(score[:]), own(score[:]), ALU.subtract))
            dve.wait_ge(earlier_ok, 1)
            step(nc.vector.scalar_tensor_tensor(out=ahead[:], in0=ahead_by[:], scalar=0.0,
                                                in1=earlier[:].rearrange("p e f -> p (e f)").unsqueeze(1).broadcast_to([P, U, E * E]),
                                                op0=ALU.is_equal, op1=ALU.mult))
            step(nc.vector.scalar_tensor_tensor(out=ahead[:], in0=ahead_by[:], scalar=0.0, in1=ahead[:],
                                                op0=ALU.is_gt, op1=ALU.add))
            step(nc.vector.reduce_sum(rank[:], four(ahead[:]), AX.X))
            step(nc.vector.scalar_tensor_tensor(out=chosen[:], in0=rank[:], scalar=1.5, in1=score[:],
                                                op0=ALU.is_lt, op1=ALU.mult))
            t1_step(1)
            step(nc.vector.reduce_sum(total[:], chosen[:], AX.X))
            step(nc.vector.tensor_scalar_add(total[:], total[:], 1e-20))
            step(nc.vector.reciprocal(total[:], total[:]))
            nc.vector.tensor_tensor(weight[:], chosen[:], wide(total[:]), ALU.mult).then_inc(weight_ok, 1)
            t1_step(2)
            for n in range(B):
                dve.wait_ge(wTh_ok, n + 1)
                nc.vector.tensor_tensor(weightT[32:32 + E, half(n)], W_BANK[n][0:E, :],
                                        weightT[0:E, half(n)].bitcast(f32), ALU.subtract).then_inc(wTl_ok, 1)

            def h_step(r):
                m, n = STEPS[WEIGHTED[r]]
                dve.wait_ge(wb_ps, r + 1)
                dve.wait_ge(t1_ok, WEIGHTED[r] + 1)
                nc.vector.tensor_tensor(hidden[:, m, half(n)], hidden[:, m, half(n)], W_BANK[r % 2][:], ALU.mult).then_inc(h_ok, 1)

            def norm_tokens(q):
                own = slice(q * QT // 2, (q + 1) * QT // 2)
                tiles_q = range(q * QT // 2, (q + 1) * QT // 2)
                dve.wait_ge(y_ps, q + 1)
                made = Y_BANK[q][:, 0:QT // 2 * C].rearrange("p (u c) -> p u c", c=C)
                nc.vector.tensor_tensor(x1[:, own, :], x_sb[:, own, :], made, ALU.add).then_inc(x1_ok, 1)
                dve.wait_ge(x1_ok, q + 1)
                for u in tiles_q:
                    last = nc.vector.bn_stats(stats[:, u, :], x1[:, u, :])
                step(last)
                for u in tiles_q:
                    last = nc.vector.bn_aggr(moments[:, u, :], stats[:, u, :])
                step(last)
                nc.vector.tensor_scalar_add(var_eps[:, own], moments[:, own, 1], EPS).then_inc(var_ok, 1)

            def scale_tokens(q):
                dve.wait_ge(rstd_ok, q + 1)
                for u in range(q * QT // 2, (q + 1) * QT // 2):
                    last = nc.vector.tensor_scalar(xn[:, u, :], x1[:, u, :], moments[:, u, 0:1], rstd[:, u:u + 1],
                                                   ALU.subtract, ALU.mult)
                last.then_inc(xn_ok, 1)

            def queries_lo(p, b, psum):
                dve.wait_ge(qhi_ok[b], p)
                if not known(p) or p > 1:
                    dve.wait_ge(q_ok[b], 96 * p - 96)
                nc.vector.scalar_tensor_tensor(out=q_lo[:, half(b)], in0=psum[:], scalar=float(D) ** -0.5,
                                               in1=q_hi[:, half(b)].bitcast(f32), op0=ALU.mult,
                                               op1=ALU.subtract).then_inc(qlo_ok[b], 1)

            def first_queries_lo(b):
                for h in range(2):
                    dve.wait_ge(first_hi, 2 * b + h + 1)
                    low = q_both[h][D:P, half(b)]
                    nc.vector.scalar_tensor_tensor(out=low, in0=FIRST_BANK[b][h][D:P, :], scalar=float(D) ** -0.5, in1=low.bitcast(f32),
                                                   op0=ALU.mult, op1=ALU.subtract).then_inc(first_lo, 1)

            def tokens_lo(n, psum):
                dve.wait_ge(xnTh_ok, n + 1)
                nc.vector.scalar_tensor_tensor(out=xnT_lo[:, half(n)], in0=psum[:], scalar=g_in_col[:, 0:1],
                                               in1=xnT_hi[:, half(n)].bitcast(f32), op0=ALU.mult,
                                               op1=ALU.subtract).then_inc(xnTl_ok, 1)

            def keys_lo(n, psum, made):
                dve.wait_ge(kh_ok, n + 1)
                nc.vector.tensor_tensor(k_lo[0:D, half(n)], psum[0:D, :], k_hi[0:D, half(n)].bitcast(f32),
                                        ALU.subtract).then_inc(kl_ok, 1)
                dve.wait_ge(v_ps, n + 1)
                made = made[:, 0:QT * VW].rearrange("p (u w) -> p u w", w=VW)
                nc.vector.tensor_copy(v_sb[:, n * QT:(n + 1) * QT, :], made[:, :, 0:D]).then_inc(v_ok, 1)
                nc.vector.scalar_tensor_tensor(
                    out=neg_null[:, n].rearrange("p h t -> p t h"), in0=made[:, :, D:VW],
                    scalar=-float(D) ** -0.5, in1=null_bias_row[:].unsqueeze(1).broadcast_to([P, QT, H]),
                    op0=ALU.mult, op1=ALU.subtract).then_inc(negnull_ok, 1)

            t1_step(3)
            h_step(0)
            t1_step(4)
            for r in range(1, 4):
                h_step(r)
            t1_step(5)
            dve.wait_ge(null_prod_ok, 1)
            nc.vector.reduce_sum(vw[:, D:VW], null_prod[:].rearrange("p (h d) -> p h d", d=D), AX.X).then_inc(wn_ok, 1)
            dve.wait_ge(ld["mask"], 16)
            nc.vector.tensor_scalar(k_lo[D:D + 1, :], keep_row[D:D + 1, :], -NEG, NEG, ALU.mult, ALU.add).then_inc(mask_ok, 1)
            dve.wait_ge(ld["null_v"], 32)
            for k in range(2):
                nc.vector.tensor_copy(place_v[k * D:(k + 1) * D, k::H + 2],
                                      null_v_col[k * D:(k + 1) * D, 0:1].broadcast_to([D, PAIRS])).then_inc(place_ok, 1)
            t1_step(6)
            norm_tokens(0)
            norm_tokens(1)
            scale_tokens(0)
            scale_tokens(1)
            t1_step(7)
            h_step(4)
            t1_step(8)
            h_step(5)
            tokens_lo(0, bank[4])
            t1_step(9)
            h_step(6)
            h_step(7)
            first_queries_lo(0)
            norm_tokens(2)
            keys_lo(0, bank[0], bank[2])
            norm_tokens(3)
            scale_tokens(2)
            scale_tokens(3)

            def score_slot(p, b, i, par, j):
                n = ordinal(p, b)
                dve.wait_ge(s_ps, SLOTS * n + i + 1)
                if any_step(p, b, 1) or i >= 2:
                    dve.wait_ge(exp_ok, NU * n + before[i] - len(UNITS[i - 1]))
                if i == 0:
                    if b == 0:
                        dve.wait_ge(bias_ok[par], QT * j + QT)
                    dve.wait_ge(null_now_ok[b], p + 1)
                stand_alone(dve, dve_passed)
                for h, t, off in UNITS[i]:
                    w = (t + 1) * P
                    r = h * QT + t
                    nc.vector.tensor_tensor_reduce(
                        out=neg_s[:, (b + i) % 2, off:off + w], in0=S_BANK[(b + i) % 2][:, off:off + w],
                        in1=bias_sb[:, par, h, at_t[t]:at_t[t] + w], scale=-1.0, scalar=neg_null_now[:, b, r:r + 1],
                        op0=ALU.add, op1=ALU.min, accum_out=neg_max[:, b, r:r + 1]).then_inc(neg_ok, 1)

            def invert(p, b):
                dve.wait_ge(sum_ok, ordinal(p, b) + 1)
                nc.vector.reciprocal(inv_sum[:, b, :], full_sum[:, b, :]).then_inc(inv_ok, 1)

            def normalise(p, b):
                dve.wait_ge(pv_ps, len(PIECES) * ordinal(p, b) + len(PIECES))
                dve.wait_ge(wide_ok, ordinal(p, b) + 1)
                nc.vector.tensor_tensor(headsT[:, half(b)], PV_BANK[:], inv_wide[:, b, :], ALU.mult).then_inc(head_ok, 1)

            def last_norm(n):
                own = slice(n * QT, (n + 1) * QT)
                dve.wait_ge(wo_ps, B * (PAIRS - 1) + n + 1)
                dve.wait_ge(null_ps, n + 1)
                for u in range(QT):
                    last = nc.vector.bn_stats(stats[:, n * QT + u, :], F_BANK[n][:, cols(u)])
                step(last)
                for u in range(n * QT, (n + 1) * QT):
                    last = nc.vector.bn_aggr(moments[:, u, :], stats[:, u, :])
                step(last)
                nc.vector.tensor_scalar_add(var_eps[:, own], moments[:, own, 1], EPS).then_inc(var_ok, 1)

            def last_centre(n):
                for u in range(n * QT, (n + 1) * QT):
                    last = nc.vector.scalar_tensor_tensor(out=normed[:, u, :], in0=F_BANK[n][:, cols(u % QT)],
                                                          scalar=moments[:, u, 0:1], in1=g_out_row[:],
                                                          op0=ALU.subtract, op1=ALU.mult)
                step(last)

            def last_scale(n):
                dve.wait_ge(rstd_ok, 2 * B + n + 1)
                for u in range(n * QT, (n + 1) * QT):
                    last = nc.vector.scalar_tensor_tensor(out=result[:, u, :], in0=normed[:, u, :], scalar=rstd[:, u:u + 1],
                                                          in1=x1[:, u, :], op0=ALU.mult, op1=ALU.add)
                    if u % 2:
                        last.then_inc(result_ok, 1)

            def body(p, par, j):
                for b in range(B):
                    for i in range(SLOTS):
                        one, two = back(p, b, 1), back(p, b, 2)
                        if not known(p) or p < PAIRS:
                            score_slot(p, b, i, par, j)
                        if known(p) and (p, b) == (0, 0):
                            if i == 0:
                                dve.wait_ge(nout_ps, 1)
                                nc.vector.tensor_copy(null_out[:], bank[7][0:H, 0:C]).then_inc(nout_ok, 1)
                                tokens_lo(1, bank[3])
                            if i == 2:
                                keys_lo(1, bank[2], bank[7])
                            if i == 3:
                                first_queries_lo(1)
                        if two and i == 1:
                            normalise(*two)
                        done = lagged(p, b, i, LAG)
                        if done and (done[1] + done[2]) % 2 == 1:
                            evacuate(dve, *done)
                        if one and i == 1:
                            invert(*one)
                        if i == 2 and (not known(p) or p + 1 < PAIRS):
                            queries_lo(p + 1, b, X_BANK)
                        if known(p) and p == PAIRS and (b, i) == (0, 4):
                            last_norm(0)
                        if known(p) and p == PAIRS and (b, i) == (1, 1):
                            last_centre(0)
                            last_scale(0)
                            last_norm(1)
                            last_centre(1)
                            last_scale(1)

            loop(nc.vector, body)

        @block.tensor
        def _(pe):
            def mm(o, a, b, start=True, stop=True, loose=False):
                return nc.tensor.matmul(o, a, b, start=start, stop=stop, skip_group_check=loose)

            def three(o, a_hi, a_lo, b_hi, b_lo):
                mm(o, a_hi, b_hi, True, False)
                mm(o, a_lo, b_hi, False, False)
                return mm(o, a_hi, b_lo, False, True)

            def keep_warm(count, psum):
                for _ in range(count):
                    mm(psum[:], zero_bf[:, 0:P], zero_bf[:])

            pe.wait_ge(warm_ok, 1)
            keep_warm(WARM, bank[7])
            pe.wait_ge(ident_ok, 1)
            pe.wait_ge(ld["x"], 16)
            for n in range(B):
                for u in range(QT):
                    last = nc.tensor.transpose(bank[n][:, cols(u)], x_sb[:, n * QT + u, :], ident[:])
                last.then_inc(xT_ps, 1)
            pe.wait_ge(ld["router"], 48)
            nc.tensor.transpose(bank[2][:, 0:E], wt_sb[:], ident[0:E, 0:E])
            nc.tensor.transpose(bank[2][0:G, E:2 * E], wg_sb[:], ident[0:E, 0:E])
            nc.tensor.transpose(bank[2][0:G, 2 * E:2 * E + B], cond_sb[:], ident[0:B, 0:B]).then_inc(small_ps, 1)

            def gate_of(s):
                m, n = STEPS[s]
                if s == 0:
                    pe.wait_ge(ld["sgate"], 16)
                    pe.wait_ge(xT_a, 1)
                if s == 1:
                    pe.wait_ge(x_lo_ok, B)
                    pe.wait_ge(w_lo_ok, 1)
                if s >= 2:
                    pe.wait_ge(sloped_ok, s - 1)
                if s == 0:
                    last = mm(GATE_BANK[0][:], gate_sb[:, m, :], xT[:, half(n)])
                else:
                    last = three(GATE_BANK[s % 2][:], gate_hi[:, m, :], gate_lo[:, m, :], xT_hi[:, half(n)], xT_lo[:, half(n)])
                last.then_inc(gate_ps, 1)

            def up_of(s):
                m, n = STEPS[s]
                if s == 0:
                    pe.wait_ge(ld["sup"], 16)
                if s == 1:
                    pe.wait_ge(w_lo_ok, 2)
                if s >= 2:
                    pe.wait_ge(t1_ok, s - 1)
                if s == 0:
                    last = mm(UP_BANK[0][:], up_sb[:, m, :], xT[:, half(n)])
                else:
                    last = three(UP_BANK[s % 2][:], up_hi[:, m, :], up_lo[:, m, :], xT_hi[:, half(n)], xT_lo[:, half(n)])
                last.then_inc(up_ps, 1)

            gate_of(0)
            pe.wait_ge(small_ok, 1)
            pe.wait_ge(xT_v, 1)
            for n in range(B):
                mm(Y_BANK[n][:, 0:QT * E].rearrange("p (u e) -> p u e", e=E), condT[:, n, :],
                   wgT[:].unsqueeze(1).broadcast_to([G, QT, E]), True, False, loose=True)
                for u in range(QT):
                    last = mm(Y_BANK[n][:, u * E:(u + 1) * E], xT[:, cols(n * QT + u)], wtT[:], False, u == QT - 1, loose=True)
            last.then_inc(logit_ps, 1)

            def weights_wide(r):
                m, n = STEPS[WEIGHTED[r]]
                pe.wait_ge(wTl_ok, B)
                if r >= 2:
                    pe.wait_ge(h_ok, r - 1)
                mm(W_BANK[r % 2][:], pick_r[:, m, :], weightT[:, half(n)]).then_inc(wb_ps, 1)

            def down(n, part):
                pe.wait_ge(h_ok, EP * (n + 1))
                if n == 0 and part == 0:
                    pe.wait_ge(ld["down"], 16)
                    pe.wait_ge(ld["sdown"], 16)
                q = 2 * n + part
                for u in range(QT // 2):
                    for m in range(NM):
                        last = mm(Y_BANK[q][:, cols(u)], hidden[:, m, cols(q * QT // 2 + u)], down_sb[:, m, :], m == 0, m == NM - 1)
                last.then_inc(y_ps, 1)

            def tokensT(n, psum):
                pe.wait_ge(xn_ok, 2 * n + 2)
                for u in range(QT):
                    last = nc.tensor.transpose(psum[:, cols(u)], xn[:, n * QT + u, :], ident[:])
                last.then_inc(xnT_ps, 1)

            def queries(p, b, par, psum):
                three(psum[:], wq_hi[:, par, :], wq_lo[:, par, :], xnT_hi[:, half(b)], xnT_lo[:, half(b)]).then_inc(q_ps[b], 1)

            def first_queries(b):
                for h in range(2):
                    w_hi, w_lo = (w[:, h].rearrange("p k d -> p (k d)") for w in (first_w_hi, first_w_lo))
                    three(FIRST_BANK[b][h][:], w_hi, w_lo, xnT_hi[:, half(b)], xnT_lo[:, half(b)]).then_inc(first_ps, 1)

            def keys(n, psum):
                three(psum[:], wk_hi[:], wk_lo[:], xnT_hi[:, half(n)], xnT_lo[:, half(n)]).then_inc(k_ps, 1)

            def values_made(n, psum):
                for u in range(QT):
                    own = cols(n * QT + u)
                    last = three(psum[:, u * VW:(u + 1) * VW], xnT_hi[:, own], xnT_lo[:, own], vw_hi[:], vw_lo[:])
                last.then_inc(v_ps, 1)

            up_of(0)
            for s in range(1, 4):
                gate_of(s)
                up_of(s)
            pe.wait_ge(weight_ok, 1)
            for n in range(B):
                for u in range(QT):
                    last = nc.tensor.transpose(W_BANK[n][0:E, cols(u)], weight[:, n * QT + u, :], ident[:])
                last.then_inc(wT_ps, 1)
            pe.wait_ge(pick_ok, 1)
            for s in range(4, 7):
                gate_of(s)
                up_of(s)
                if s < 6:
                    weights_wide(2 * s - 8)
                    weights_wide(2 * s - 7)
            down(0, 0)
            down(0, 1)
            gate_of(7)
            up_of(7)
            weights_wide(4)
            gate_of(8)
            up_of(8)
            tokensT(0, bank[4])
            weights_wide(5)
            gate_of(9)
            up_of(9)
            weights_wide(6)
            weights_wide(7)
            pe.wait_ge(xnTl_ok, 1)
            pe.wait_ge(first_w_ok, 2)
            first_queries(0)
            down(1, 0)
            pe.wait_ge(sloped_ok, len(STEPS))
            pe.wait_ge(wkv_split_ok, 3)
            keys(0, bank[0])
            values_made(0, bank[2])
            down(1, 1)

            def scores(p, b, i):
                n = ordinal(p, b)
                if i == 0:
                    if known(p) and p == 0:
                        pe.wait_ge(first_one, 2 * b + 2)
                        pe.wait_ge(first_lo, 2 * b + 2)
                    else:
                        pe.wait_ge(q_ok[b], 96 * p)
                if any_step(p, b, 1) or i >= 2:
                    pe.wait_ge(neg_ok, NU * n + before[i] - len(UNITS[i - 1]))
                for h, t, off in UNITS[i]:
                    w = (t + 1) * P
                    o = S_BANK[(b + i) % 2][:, off:off + w]
                    mm(o, q_both[h][:, cols(b * QT + t)], k_hi[:, b * S:b * S + w], True, False)
                    last = mm(o, q_one[h][:, cols(b * QT + t)], k_lo[:, b * S:b * S + w], False, True)
                last.then_inc(s_ps, 1)

            def transposes(p, b, i):
                n = ordinal(p, b)
                pe.wait_ge(exp_ok, NU * n + before[3 if i < 2 else SLOTS])
                if any_step(p, b, 1) or i >= 2:
                    evacuated(pe, *lagged_any(p, b, i, 2))
                for c, (h, t, k) in enumerate(BLOCKS[i]):
                    at = at_t[t] + k * P
                    last = nc.tensor.transpose(T_BANK[(b + i) % 2][:, cols(c)], probs[:, b, h, at:at + P], ident[:])
                last.then_inc(t_ps, 1)

            def lagged_any(p, b, i, slots):
                d = (slots - i + SLOTS - 1) // SLOTS
                return p - (d + 1 - b) // 2, (b + d) % 2, i - slots + d * SLOTS

            def weigh_values(p, b, piece):
                n = ordinal(p, b)
                tiles_k, banks = PIECES[piece]
                for i in banks:
                    evacuated(pe, p, b, i)
                if piece == 0 and any_step(p, b, 1):
                    pe.wait_ge(head_ok, n)
                for k in tiles_k:
                    w = (QT - k) * P
                    for h in range(2):
                        last = mm(PV_BANK[h * D:(h + 1) * D, k * P:S], v_sb[:, b * QT + k, :],
                                  probsT[:, b, h, at_j[k]:at_j[k] + w], k == 0, k == 2, loose=True)
                last.then_inc(pv_ps, 1)

            def inverse_T(p, b):
                n = ordinal(p, b)
                if not known(p) or n + 1 < B * (PAIRS - 1):
                    at, c = (p, 1) if b == 0 else (p + 1, 0)
                    pe.wait_ge(qlo_ok[c], at + 1)
                else:
                    pe.wait_ge(wide_ok, n)
                pe.wait_ge(inv_split_ok, ordinal(p, b) + 1)
                nc.tensor.transpose(X_BANK[0:2 * R, 0:P], inv_split[:, b, :].bitcast(f32), ident[:]).then_inc(invT_ps, 1)

            def inverse_wide(p, b):
                pe.wait_ge(invT_ok, ordinal(p, b) + 1)
                if known(p) and ordinal(p, b) == 0:
                    pe.wait_ge(row_of_ok, 1)
                for t in range(QT):
                    last = mm(X_BANK[:, cols(t)], row_of_r[:, t, :], inv_T[:, b, :])
                last.then_inc(wide_ps, 1)

            def project(p, b):
                pe.wait_ge(head_ok, ordinal(p, b) + 1)
                for u in range(QT):
                    last = mm(F_BANK[b][:, cols(u)], headsT[:, cols(b * QT + u)], wo_sb[:, bass.ds(p * C, C)],
                              False, False, loose=True)
                last.then_inc(wo_ps, 1)

            def null_T(n):
                pe.wait_ge(nullp_ok, B * PAIRS - B + n + 1)
                pe.wait_ge(neg_ok, NU * B * PAIRS - (0 if n else len(UNITS[SLOTS - 1])))
                for u in range(QT):
                    last = nc.tensor.transpose(S_BANK[n][0:H, cols(u)], null_prob[:, n * QT + u, :], ident[:])
                last.then_inc(npT_ps, 1)

            def null_share(n):
                pe.wait_ge(npT_ok, n + 1)
                for u in range(QT):
                    last = mm(F_BANK[n][:, cols(u)], null_probT[:, cols(n * QT + u)], null_out[:], False, False, loose=True)
                last.then_inc(null_ps, 1)

            pe.wait_ge(kl_ok, 1)
            pe.wait_ge(mask_ok, 1)
            pe.wait_ge(zero_ok, 2)

            def second_batch(i):
                if i == 1:
                    pe.wait_ge(place_ok, 2)
                    pe.wait_ge(ld["wo"], 16)
                    pe.wait_ge(x1_ok, 2 * B)
                    for a in range(PAIRS):
                        last = mm(bank[7][0:H, 0:C], place_v[:, a * H:(a + 1) * H], wo_sb[:, a * C:(a + 1) * C],
                                  a == 0, a == PAIRS - 1)
                    last.then_inc(nout_ps, 1)
                    tokensT(1, bank[3])
                if i == 2:
                    pe.wait_ge(xnTl_ok, 2)
                    pe.wait_ge(v_ok, 1)
                    pe.wait_ge(negnull_ok, 1)
                    keys(1, bank[2])
                    pe.wait_ge(nout_ok, 1)
                    values_made(1, bank[7])
                if i == 3:
                    pe.wait_ge(first_one, 2)
                    pe.wait_ge(first_lo, 2)
                    first_queries(1)
                    pe.wait_ge(kl_ok, B)

            def body(p, par, j):
                for b in range(B):
                    for i in range(SLOTS):
                        one, two = back(p, b, 1), back(p, b, 2)
                        if not known(p) or p < PAIRS:
                            scores(p, b, i)
                        done = lagged(p, b, i, LAG)
                        drain = known(p) and p == PAIRS
                        if i == (2 if drain else 3) and two and not (drain and b == 1):
                            project(*two)
                        if known(p) and (p, b) == (0, 0):
                            second_batch(i)
                        if done:
                            transposes(*done)
                        if drain and (b, i) == (0, 3):
                            inverse_T(*one)
                        if drain and (b, i) == (0, 4):
                            inverse_wide(*one)
                        if i >= 3 and one:
                            weigh_values(*one, i - 3)
                        if i == 0 and two:
                            weigh_values(*two, 2)
                        if i == 1 and (not known(p) or p + 1 < PAIRS):
                            pe.wait_ge(wq_split, p + 1)
                            if any_step(p, b, 2):
                                pe.wait_ge(wide_ok, ordinal(p, b) - 1)
                            else:
                                pe.wait_ge(first_one, 2)
                                pe.wait_ge(first_lo, 2)
                            queries(p + 1, b, 1 - par, X_BANK)
                        if drain and (b, i) == (0, 1):
                            null_T(0)
                        if drain and (b, i) == (0, 3):
                            null_share(0)
                        if i == 3 and one and not drain:
                            inverse_T(*one)
                        if drain and (b, i) == (0, 4):
                            null_T(1)
                        if i == 4 and one and not drain:
                            inverse_wide(*one)
                        if drain and (b, i) == (1, 0):
                            null_share(1)
                            project(*two)
                        if known(p) and p == 0 and b == 1:
                            if i == 4:
                                pe.wait_ge(v_ok, B)
                                pe.wait_ge(negnull_ok, B)
                                for n in range(B):
                                    mm(F_BANK[n][:], zero_bf[:, 0:P], zero_bf[:], True, False, loose=True).then_inc(fin_zero, 1)

            loop(nc.tensor, body)


_INS = ["x", "cond_64", "fside_16xSxS_0", "mask_BxS_bk0", "L0_cond_wt", "L0_cond_wg", "L0_cond_w_gate", "L0_cond_w_up",
        "L0_cond_w_down", "L0_cond_sw_gate", "L0_cond_sw_up", "L0_cond_sw_down", "L1_cond_g_in",
        "L1_cond_null_attn_bias", "L1_cond_Wq", "L1_cond_Wkv", "L1_cond_Wo", "L1_cond_g_out"]


def kernel(**inputs):
    import numpy as np
    import concourse.bacc as bacc
    from concourse.bass_utils import run_bass_kernel_spmd as run

    nc = bacc.Bacc("TRN2", target_bir_lowering=False, num_devices=1)
    arrays, args = {}, []
    for name in _INS:
        a = np.ascontiguousarray(inputs[name])
        arrays[name + "_dram"] = a
        args.append(nc.dram_tensor(name + "_dram", a.shape, mybir.dt.from_np(a.dtype), kind="ExternalInput").ap())
    x = inputs["x"]
    args.append(nc.dram_tensor("out_dram", tuple(x.shape), mybir.dt.float32, kind="ExternalOutput").ap())
    moe_then_attention_program(nc, *args)
    r = run(nc, [arrays], core_ids=[0])
    return r.results[0]["out_dram"]
```
